# Optimizing a Trainium2 kernel written in Bass

```python
import numpy as np
import jax
import jax.numpy as jnp

def _softmax(x, axis=-1):
    return jax.nn.softmax(x, axis=axis)

def _gelu(x):
    return jax.nn.gelu(x, approximate=True)

def _silu(x):
    return jax.nn.silu(x)

def _sigmoid(x):
    return jax.nn.sigmoid(x)

def _layernorm(x, axis=-1, eps=1e-05):
    m = jnp.mean(x, axis=axis, keepdims=True)
    v = jnp.var(x, axis=axis, keepdims=True)
    return (x - m) / jnp.sqrt(v + eps)

def _scatter_add(tgt, idx, src, axis=0):
    return tgt.at[idx].add(src)

def _segment_sum(src, seg, n):
    return jax.ops.segment_sum(src, seg, n)
kernel_name = 'mk_adaln_d2_jaxref_r8_821e76'

def setup_inputs(seed: int=0):
    np.random.seed(seed)
    _w = jnp.asarray

    def _L0_attn_setup():
        import jax, jax.numpy as jnp
        import numpy as np
        HEADS = 32
        DIM_HEAD = 32
        EPS = 1e-06
        key = jax.random.key(seed)
        k1, k2, k3 = jax.random.split(key, 3)
        b, n, dim = (2, 256, 128)
        x = jax.random.normal(k1, (b, n, dim), dtype=jnp.float32)
        w_qkv = jax.random.normal(k2, (dim, 3 * HEADS * DIM_HEAD), dtype=jnp.float32) * dim ** (-0.5)
        w_out = jax.random.normal(k3, (HEADS * DIM_HEAD, dim), dtype=jnp.float32) * dim ** (-0.5)
        b_out = jnp.zeros((dim,), dtype=jnp.float32)
        ln_gamma = jnp.ones((dim,), dtype=jnp.float32)
        ln_beta = jnp.zeros((dim,), dtype=jnp.float32)
        return {'x': x, 'w_qkv': w_qkv, 'w_out': w_out, 'b_out': b_out, 'ln_gamma': ln_gamma, 'ln_beta': ln_beta}
    _L0_attn_in = _L0_attn_setup()

    def _L0_ffn_setup():
        import jax, jax.numpy as jnp
        import numpy as np
        B, S, H, F, E, K = (2, 256, 128, 512, 8, 2)

        def _init_w(key, shape, fan_in):
            return jax.random.normal(key, shape, jnp.float32) * fan_in ** (-0.5)

        def _ffn(x, wi, bi, wo, bo):
            return jax.nn.selu(x @ wi + bi) @ wo + bo
        key = jax.random.key(seed)
        ks = jax.random.split(key, 6)
        return {'x': jax.random.normal(ks[0], (B, S, H), jnp.float32), 'gate_wi': _init_w(ks[1], (H, F), H), 'gate_bi': jnp.zeros((F,), jnp.float32), 'gate_wo': _init_w(ks[2], (F, H), F), 'gate_bo': jnp.zeros((H,), jnp.float32), 'exp_wi': _init_w(ks[3], (E, H, F), H), 'exp_bi': jnp.zeros((E, F), jnp.float32), 'exp_wo': _init_w(ks[4], (E, F, H), F), 'exp_bo': jnp.zeros((E, H), jnp.float32)}
    _L0_ffn_in = _L0_ffn_setup()
    _L0_c = _w((lambda *s: np.random.randn(*s).astype(np.float32) * 0.05)(4, 128))
    _L0_wmod = _w((lambda *s: np.random.randn(*s).astype(np.float32) * 0.05)(128, 6 * 128) * 128 ** (-0.5))

    def _L1_attn_setup():
        import jax, jax.numpy as jnp
        import numpy as np
        B, S, D, H, L, F = (4, 256, 128, 16, 8, 512)
        DH = D // H

        def _ln(x, g, b):
            m = jnp.mean(x, axis=-1, keepdims=True)
            v = jnp.mean((x - m) ** 2, axis=-1, keepdims=True)
            return (x - m) * jax.lax.rsqrt(v + 1e-05) * g + b

        def _phi(t):
            return jax.nn.elu(t) + 1.0
        key = jax.random.key(seed)
        ks = jax.random.split(key, 12)
        s = 0.02
        n = jax.random.normal
        return {'x': n(ks[0], (B, S, D), jnp.float32), 'Wq': n(ks[1], (L, D, D), jnp.float32) * s, 'bq': jnp.zeros((L, D), jnp.float32), 'Wk': n(ks[2], (L, D, D), jnp.float32) * s, 'bk': jnp.zeros((L, D), jnp.float32), 'Wv': n(ks[3], (L, D, D), jnp.float32) * s, 'bv': jnp.zeros((L, D), jnp.float32), 'Wo': n(ks[4], (L, D, D), jnp.float32) * s, 'bo': jnp.zeros((L, D), jnp.float32), 'g1': jnp.ones((L, D), jnp.float32), 'be1': jnp.zeros((L, D), jnp.float32), 'g2': jnp.ones((L, D), jnp.float32), 'be2': jnp.zeros((L, D), jnp.float32), 'W1': n(ks[5], (L, D, F), jnp.float32) * s, 'c1': jnp.zeros((L, F), jnp.float32), 'W2': n(ks[6], (L, F, D), jnp.float32) * s, 'c2': jnp.zeros((L, D), jnp.float32), 'gf': jnp.ones((D,), jnp.float32), 'bef': jnp.zeros((D,), jnp.float32)}
    _L1_attn_in = _L1_attn_setup()

    def _L1_ffn_setup():
        import jax, jax.numpy as jnp
        import numpy as np
        TOP_K = 2

        def _ffn(x, gw, uw, dw):
            return jax.nn.silu(x @ gw.T) * (x @ uw.T) @ dw.T
        key = jax.random.key(seed)
        ks = jax.random.split(key, 8)
        w = lambda k, shape: jax.random.normal(k, shape, jnp.float32) * 0.02
        return dict(x=jax.random.normal(ks[0], (4, 256, 128), jnp.float32), gate_w=w(ks[1], (8, 128)), expert_gate=w(ks[2], (8, 352, 128)), expert_up=w(ks[3], (8, 352, 128)), expert_down=w(ks[4], (8, 128, 352)), shared_gate=w(ks[5], (352, 128)), shared_up=w(ks[6], (352, 128)), shared_down=w(ks[7], (128, 352)))
    _L1_ffn_in = _L1_ffn_setup()
    _L1_c = _w((lambda *s: np.random.randn(*s).astype(np.float32) * 0.05)(4, 128))
    _L1_wmod = _w((lambda *s: np.random.randn(*s).astype(np.float32) * 0.05)(128, 6 * 128) * 128 ** (-0.5))
    _d = {'L0_attn_x': _L0_attn_in['x'], 'L0_attn_w_qkv': _L0_attn_in['w_qkv'], 'L0_attn_w_out': _L0_attn_in['w_out'], 'L0_attn_b_out': _L0_attn_in['b_out'], 'L0_attn_ln_gamma': _L0_attn_in['ln_gamma'], 'L0_attn_ln_beta': _L0_attn_in['ln_beta'], 'L0_ffn_gate_wi': _L0_ffn_in['gate_wi'], 'L0_ffn_gate_bi': _L0_ffn_in['gate_bi'], 'L0_ffn_gate_wo': _L0_ffn_in['gate_wo'], 'L0_ffn_gate_bo': _L0_ffn_in['gate_bo'], 'L0_ffn_exp_wi': _L0_ffn_in['exp_wi'], 'L0_ffn_exp_bi': _L0_ffn_in['exp_bi'], 'L0_ffn_exp_wo': _L0_ffn_in['exp_wo'], 'L0_ffn_exp_bo': _L0_ffn_in['exp_bo'], 'L0_c': _L0_c, 'L0_wmod': _L0_wmod, 'L1_attn_Wq': _L1_attn_in['Wq'], 'L1_attn_bq': _L1_attn_in['bq'], 'L1_attn_Wk': _L1_attn_in['Wk'], 'L1_attn_bk': _L1_attn_in['bk'], 'L1_attn_Wv': _L1_attn_in['Wv'], 'L1_attn_bv': _L1_attn_in['bv'], 'L1_attn_Wo': _L1_attn_in['Wo'], 'L1_attn_bo': _L1_attn_in['bo'], 'L1_attn_g1': _L1_attn_in['g1'], 'L1_attn_be1': _L1_attn_in['be1'], 'L1_attn_g2': _L1_attn_in['g2'], 'L1_attn_be2': _L1_attn_in['be2'], 'L1_attn_W1': _L1_attn_in['W1'], 'L1_attn_c1': _L1_attn_in['c1'], 'L1_attn_W2': _L1_attn_in['W2'], 'L1_attn_c2': _L1_attn_in['c2'], 'L1_attn_gf': _L1_attn_in['gf'], 'L1_attn_bef': _L1_attn_in['bef'], 'L1_ffn_gate_w': _L1_ffn_in['gate_w'], 'L1_ffn_expert_gate': _L1_ffn_in['expert_gate'], 'L1_ffn_expert_up': _L1_ffn_in['expert_up'], 'L1_ffn_expert_down': _L1_ffn_in['expert_down'], 'L1_ffn_shared_gate': _L1_ffn_in['shared_gate'], 'L1_ffn_shared_up': _L1_ffn_in['shared_up'], 'L1_ffn_shared_down': _L1_ffn_in['shared_down'], 'L1_c': _L1_c, 'L1_wmod': _L1_wmod}
    _x0 = _d['L0_attn_x']
    _d['L0_attn_x'] = jax.random.normal(jax.random.fold_in(jax.random.key(seed), 1), (4, 512, 128), dtype=_x0.dtype)
    del _x0
    return _d

def reference(L0_attn_x, L0_attn_w_qkv, L0_attn_w_out, L0_attn_b_out, L0_attn_ln_gamma, L0_attn_ln_beta, L0_ffn_gate_wi, L0_ffn_gate_bi, L0_ffn_gate_wo, L0_ffn_gate_bo, L0_ffn_exp_wi, L0_ffn_exp_bi, L0_ffn_exp_wo, L0_ffn_exp_bo, L0_c, L0_wmod, L1_attn_Wq, L1_attn_bq, L1_attn_Wk, L1_attn_bk, L1_attn_Wv, L1_attn_bv, L1_attn_Wo, L1_attn_bo, L1_attn_g1, L1_attn_be1, L1_attn_g2, L1_attn_be2, L1_attn_W1, L1_attn_c1, L1_attn_W2, L1_attn_c2, L1_attn_gf, L1_attn_bef, L1_ffn_gate_w, L1_ffn_expert_gate, L1_ffn_expert_up, L1_ffn_expert_down, L1_ffn_shared_gate, L1_ffn_shared_up, L1_ffn_shared_down, L1_c, L1_wmod):

    def _L0_attn_ref(x, w_qkv, w_out, b_out, ln_gamma, ln_beta):
        import jax, jax.numpy as jnp
        import numpy as np
        HEADS = 32
        DIM_HEAD = 32
        EPS = 1e-06
        b, n, dim = x.shape
        scale = DIM_HEAD ** (-0.5)
        qkv = x @ w_qkv
        qkv = qkv.reshape(b, n, 3, HEADS, DIM_HEAD)
        qkv = jnp.transpose(qkv, (2, 0, 3, 1, 4))
        q, k, v = (qkv[0], qkv[1], qkv[2])
        dots = jnp.einsum('bhnd,bhmd->bhnm', q, k) * scale
        attn = jax.nn.softmax(dots, axis=-1)
        out = jnp.einsum('bhnm,bhmd->bhnd', attn, v)
        out = jnp.transpose(out, (0, 2, 1, 3)).reshape(b, n, HEADS * DIM_HEAD)
        out = out @ w_out + b_out
        mu = jnp.mean(out, axis=-1, keepdims=True)
        var = jnp.mean((out - mu) ** 2, axis=-1, keepdims=True)
        out = (out - mu) / jnp.sqrt(var + EPS) * ln_gamma + ln_beta
        return out

    def _L0_ffn_ref(x, gate_wi, gate_bi, gate_wo, gate_bo, exp_wi, exp_bi, exp_wo, exp_bo):
        import jax, jax.numpy as jnp
        import numpy as np
        B, S, H, F, E, K = (2, 256, 128, 512, 8, 2)

        def _init_w(key, shape, fan_in):
            return jax.random.normal(key, shape, jnp.float32) * fan_in ** (-0.5)

        def _ffn(x, wi, bi, wo, bo):
            return jax.nn.selu(x @ wi + bi) @ wo + bo
        Bb, Ss, Hh = x.shape
        xf = x.reshape(-1, Hh)
        gate_logits = _ffn(xf, gate_wi, gate_bi, gate_wo, gate_bo)
        topv, topi = jax.lax.top_k(gate_logits, K)
        topv = topv / jnp.sum(topv, axis=-1, keepdims=True)
        onehot = (topi[..., None] == jnp.arange(E)).astype(x.dtype)
        w = jnp.einsum('nk,nke->ne', topv, onehot)
        h = jax.nn.selu(jnp.einsum('nh,ehf->enf', xf, exp_wi) + exp_bi[:, None, :])
        out_e = jnp.einsum('enf,efh->enh', h, exp_wo) + exp_bo[:, None, :]
        out = jnp.einsum('enh,ne->nh', out_e, w)
        return out.reshape(Bb, Ss, Hh)

    def _L1_attn_ref(x, Wq, bq, Wk, bk, Wv, bv, Wo, bo, g1, be1, g2, be2, W1, c1, W2, c2, gf, bef):
        import jax, jax.numpy as jnp
        import numpy as np
        B, S, D, H, L, F = (4, 256, 128, 16, 8, 512)
        DH = D // H

        def _ln(x, g, b):
            m = jnp.mean(x, axis=-1, keepdims=True)
            v = jnp.mean((x - m) ** 2, axis=-1, keepdims=True)
            return (x - m) * jax.lax.rsqrt(v + 1e-05) * g + b

        def _phi(t):
            return jax.nn.elu(t) + 1.0
        b, s, d = x.shape

        def layer(h, p):
            wq, bq_, wk, bk_, wv, bv_, wo, bo_, g1_, be1_, g2_, be2_, w1, c1_, w2, c2_ = p
            q = _phi((h @ wq + bq_).reshape(b, s, H, DH))
            k = _phi((h @ wk + bk_).reshape(b, s, H, DH))
            v = (h @ wv + bv_).reshape(b, s, H, DH)
            kv = jnp.einsum('bshd,bshm->bhdm', k, v)
            z = 1.0 / (jnp.einsum('bshd,bhd->bsh', q, k.sum(axis=1)) + 1e-06)
            att = jnp.einsum('bshd,bhdm,bsh->bshm', q, kv, z).reshape(b, s, d)
            h = h + att @ wo + bo_
            h = _ln(h, g1_, be1_)
            y = jax.nn.gelu(h @ w1 + c1_, approximate=False) @ w2 + c2_
            return (_ln(h + y, g2_, be2_), None)
        params = (Wq, bq, Wk, bk, Wv, bv, Wo, bo, g1, be1, g2, be2, W1, c1, W2, c2)
        h, _ = jax.lax.scan(layer, x, params)
        return _ln(h, gf, bef)

    def _L1_ffn_ref(x, gate_w, expert_gate, expert_up, expert_down, shared_gate, shared_up, shared_down):
        import jax, jax.numpy as jnp
        import numpy as np
        TOP_K = 2

        def _ffn(x, gw, uw, dw):
            return jax.nn.silu(x @ gw.T) * (x @ uw.T) @ dw.T
        B, S, H = x.shape
        xf = x.reshape(-1, H)
        T = xf.shape[0]
        E = expert_gate.shape[0]
        shared = _ffn(xf, shared_gate, shared_up, shared_down)
        logits = xf @ gate_w.T
        probs = jax.nn.softmax(logits, axis=-1)
        topw, topi = jax.lax.top_k(probs, TOP_K)
        topw = topw / (topw.sum(-1, keepdims=True) + 1e-20)
        comb = jnp.zeros((T, E), xf.dtype).at[jnp.arange(T)[:, None], topi].add(topw)

        def body(acc, ws):
            gw, uw, dw, wcol = ws
            return (acc + _ffn(xf, gw, uw, dw) * wcol[:, None], None)
        routed, _ = jax.lax.scan(body, jnp.zeros_like(xf), (expert_gate, expert_up, expert_down, comb.T))
        return (shared + routed).reshape(B, S, H)
    x = L0_attn_x
    mod = (_silu(L0_c) @ L0_wmod).reshape(L0_c.shape[0], 6, 1, -1)
    sa, ca, ga, sb, cb, gb = (mod[:, 0], mod[:, 1], mod[:, 2], mod[:, 3], mod[:, 4], mod[:, 5])
    ga = (2 * (ga >= 0) - 1) * jnp.maximum(jnp.abs(ga), 0.25)
    gb = (2 * (gb >= 0) - 1) * jnp.maximum(jnp.abs(gb), 0.25)
    h = _layernorm(x, axis=-1) * (1 + ca) + sa
    x = x + ga * _L0_attn_ref(h, L0_attn_w_qkv, L0_attn_w_out, L0_attn_b_out, L0_attn_ln_gamma, L0_attn_ln_beta)
    h = _layernorm(x, axis=-1) * (1 + cb) + sb
    x = x + gb * _L0_ffn_ref(h, L0_ffn_gate_wi, L0_ffn_gate_bi, L0_ffn_gate_wo, L0_ffn_gate_bo, L0_ffn_exp_wi, L0_ffn_exp_bi, L0_ffn_exp_wo, L0_ffn_exp_bo)
    mod = (_silu(L1_c) @ L1_wmod).reshape(L1_c.shape[0], 6, 1, -1)
    sa, ca, ga, sb, cb, gb = (mod[:, 0], mod[:, 1], mod[:, 2], mod[:, 3], mod[:, 4], mod[:, 5])
    ga = (2 * (ga >= 0) - 1) * jnp.maximum(jnp.abs(ga), 0.25)
    gb = (2 * (gb >= 0) - 1) * jnp.maximum(jnp.abs(gb), 0.25)
    h = _layernorm(x, axis=-1) * (1 + ca) + sa
    x = x + ga * _L1_attn_ref(h, L1_attn_Wq, L1_attn_bq, L1_attn_Wk, L1_attn_bk, L1_attn_Wv, L1_attn_bv, L1_attn_Wo, L1_attn_bo, L1_attn_g1, L1_attn_be1, L1_attn_g2, L1_attn_be2, L1_attn_W1, L1_attn_c1, L1_attn_W2, L1_attn_c2, L1_attn_gf, L1_attn_bef)
    h = _layernorm(x, axis=-1) * (1 + cb) + sb
    x = x + gb * _L1_ffn_ref(h, L1_ffn_gate_w, L1_ffn_expert_gate, L1_ffn_expert_up, L1_ffn_expert_down, L1_ffn_shared_gate, L1_ffn_shared_up, L1_ffn_shared_down)
    return x

_drawn_inputs = setup_inputs


def setup_inputs(seed=0):
    import zlib

    import numpy as np

    out = dict(_drawn_inputs(seed))
    spreads = {'L0_attn_b_out': (0.0, 0.1),
     'L0_attn_ln_gamma': (1.0, 0.2),
     'L0_attn_ln_beta': (0.0, 0.283),
     'L0_ffn_gate_bi': (0.0, 0.292),
     'L0_ffn_gate_bo': (0.0, 0.491),
     'L0_ffn_exp_bi': (0.0, 0.8),
     'L0_ffn_exp_bo': (0.0, 0.8),
     'L1_attn_bq': (0.0, 2.0),
     'L1_attn_bk': (0.0, 2.0),
     'L1_attn_bv': (0.0, 0.479),
     'L1_attn_bo': (0.0, 0.1),
     'L1_attn_g1': (1.0, 0.2),
     'L1_attn_be1': (0.0, 0.1),
     'L1_attn_g2': (1.0, 0.2),
     'L1_attn_be2': (0.0, 0.1),
     'L1_attn_c1': (0.0, 0.585),
     'L1_attn_c2': (0.0, 0.1),
     'L1_attn_gf': (1.0, 0.2),
     'L1_attn_bef': (0.0, 0.375)}
    factors = {'L1_attn_Wq': 8.0,
     'L1_attn_Wk': 8.0,
     'L1_attn_Wv': 6.169,
     'L1_attn_Wo': 4.2,
     'L1_ffn_gate_w': 8.0,
     'L1_ffn_expert_gate': 8.0,
     'L1_ffn_expert_up': 8.0,
     'L1_ffn_expert_down': 8.0,
     'L1_ffn_shared_gate': 8.0,
     'L1_ffn_shared_up': 8.0,
     'L1_ffn_shared_down': 8.0}
    for name, (base, spread) in spreads.items():
        noise = np.random.default_rng([zlib.crc32(name.encode()), seed]).standard_normal(out[name].shape)
        drawn = base * np.exp(spread * noise) if base else spread * noise
        out[name] = jnp.asarray(drawn.astype(out[name].dtype))
    for name, factor in factors.items():
        out[name] = (out[name] * factor).astype(out[name].dtype)
    return out
```

```python
from contextlib import ExitStack

import numpy as np

import concourse.bass as bass
from concourse import mybir

F32 = mybir.dt.float32
F32R = mybir.dt.float32r
U32 = mybir.dt.uint32
ALU = mybir.AluOpType
ACT = mybir.ActivationFunctionType
AX = mybir.AxisListType.X

P = 128
B, S, D = 4, 512, 128
NT = S // P

HEADS, DH = 32, 32
HC = P // DH
NC = HEADS // HC
SCALE = DH ** -0.5
E = 8
FF0 = 512
FC = FF0 // P
SELU_L = 1.0507009873554805
SELU_A = 1.6732632423543772
LAYERS, LH = 8, 16
LD = D // LH
LFF = 512
LFC = LFF // P
U = 1 + E
FF1 = 352
FCH = [(0, 128), (128, 128), (256, 96)]

BO0, GAM0, BET0, GBI, EBI, GF, BEF, C0, C1 = 0, 1, 2, 3, 7, 39, 40, 41, 45
VECS = 49
IDENT, BLOCKS, HSEL, IOTA, ONES = 0, 128, 256, 272, 280
CONSTS = 312
WQ, WKV, WO, W1, W2 = 0, 128, 384, 512, 1024
LV = 1536
BQ, LBO, LG1, LBE1, LG2, LBE2, LC1, LC2 = LV, LV + 1, LV + 2, LV + 3, LV + 4, LV + 5, LV + 6, LV + 10
LW = LV + 11
SA, CA, GG, GB, SB, CB, GX = range(7)
NM = 7


def build(nc, ins, out):
    x_in, vecs_in, consts_in, wmod_in, wqkv_in, wout_in = (ins[k] for k in ("x", "vecs", "consts", "wmod", "wqkv", "wout"))
    gwi_in, gwo_in, gbo_in, ewi_in, ewo_in, ebo_in = (ins[k] for k in ("gwi", "gwo", "gbo", "ewi", "ewo", "ebo"))
    lw_in, bkv_in, rw_in, gu_in, dn_in = (ins[k] for k in ("lw", "bkv", "rw", "gu", "dn"))

    x_tok = x_in.rearrange("b (t p) d -> b p t d", p=P)
    out_tok = out.rearrange("b (t p) d -> b p t d", p=P)

    with ExitStack() as ctx:
        def sb(name, shape, dt=F32, at=ctx):
            return at.enter_context(nc.sbuf_tensor(name, shape, dt))

        def sem(name, at=ctx):
            return at.enter_context(nc.semaphore(name))

        ps = ctx.enter_context(nc.psum_tensor("ps", [P, 8, 512], F32))
        consts = sb("consts", [P, CONSTS])
        vecs = sb("vecs", [P, VECS])
        mods = sb("mods", [P, 2, NM, B])
        nhalf = sb("nhalf", [P, NT])
        xT = sb("xT", [P, B, S])
        dve_passed, sp_passed, pool_passed = sem("dve_passed"), sem("sp_passed"), sem("pool_passed")
        ident = consts[:, IDENT:IDENT + P]

        setup(nc, locals())
        block0(nc, locals())
        rw = sb("rw", [P, E])
        gu = sb("gu", [P, U, 2, FF1])
        dn1 = sb("dn1", [P, len(FCH), U, D])
        w1_in = sem("experts1_landed")
        layers(nc, locals())
        experts1(nc, locals())


def setup(nc, g):
    ps, consts, vecs, mods, nhalf = g["ps"], g["consts"], g["vecs"], g["mods"], g["nhalf"]
    with ExitStack() as ctx:
        wmod = ctx.enter_context(nc.sbuf_tensor("wmod_sb", [P, 2, 6 * D], F32))
        sc = ctx.enter_context(nc.sbuf_tensor("silu_c", [P, 2, B], F32))
        raw = ctx.enter_context(nc.sbuf_tensor("mod_raw", [P, 2, 6, B], F32))
        gate = ctx.enter_context(nc.sbuf_tensor("gate_abs", [P, 2, 2, B], F32))
        sign = ctx.enter_context(nc.sbuf_tensor("gate_sign", [P, 2, 2, B], F32))
        small_in = ctx.enter_context(nc.semaphore("small_in"))
        wmod_in = ctx.enter_context(nc.semaphore("wmod_landed"))
        silu_done = ctx.enter_context(nc.semaphore("silu_done"))
        mod_full = ctx.enter_context(nc.semaphore("mod_full"))
        chain = ctx.enter_context(nc.semaphore("setup_chain"))
        block = ctx.enter_context(nc.Block())

        @block.sync
        def _(sp):
            sp.dma_start(vecs[:], g["vecs_in"]).then_inc(small_in, 16)
            sp.dma_start(wmod[:], g["wmod_in"]).then_inc(wmod_in, 16)
            sp.dma_start(consts[:], g["consts_in"]).then_inc(small_in, 16)

        @block.scalar
        def _(act):
            act.wait_ge(small_in, 32)
            nc.scalar.activation(sc[:].rearrange("p l b -> p (l b)"), vecs[:, C0:C0 + 2 * B],
                                 ACT.Silu).then_inc(silu_done, 1)

        @block.tensor
        def _(pe):
            pe.wait_ge(silu_done, 1)
            pe.wait_ge(wmod_in, 16)
            for lv in range(2):
                for k in range(6):
                    at = (lv * 6 + k) * B
                    mm = nc.tensor.matmul(ps[:, 0, at:at + B], wmod[:, lv, k * D:(k + 1) * D],
                                          sc[:, lv, :], start=True, stop=True)
            mm.then_inc(mod_full, 1)

        @block.vector
        def _(dve):
            n = [0]

            def then(ins):
                n[0] += 1
                ins.then_inc(chain, 1)
                dve.wait_ge(chain, n[0])

            nc.vector.memset(nhalf[:], -0.5)
            dve.wait_ge(mod_full, 1)
            then(nc.vector.tensor_copy(raw[:].rearrange("p l k b -> p (l k b)"), ps[:, 0, 0:12 * B]))
            for lv in range(2):
                ga = raw[:, lv, 2:6:3, :]
                then(nc.vector.tensor_scalar(gate[:, lv], ga, -1.0, None, ALU.mult))
                then(nc.vector.tensor_tensor(gate[:, lv], gate[:, lv], ga, ALU.max))
                then(nc.vector.tensor_scalar(gate[:, lv], gate[:, lv], 0.25, None, ALU.max))
                then(nc.vector.tensor_scalar(sign[:, lv], ga, 0.0, 2.0, ALU.is_ge, ALU.mult))
                then(nc.vector.tensor_scalar(sign[:, lv], sign[:, lv], -1.0, None, ALU.add))
                then(nc.vector.tensor_tensor(gate[:, lv], gate[:, lv], sign[:, lv], ALU.mult))
                dve.wait_ge(small_in, 32)
                gamma, beta = ((GAM0, BET0), (GF, BEF))[lv]
                nc.vector.tensor_scalar(mods[:, lv, GG, :], gate[:, lv, 0, :], vecs[:, gamma:gamma + 1], None, ALU.mult)
                nc.vector.tensor_scalar(mods[:, lv, GB, :], gate[:, lv, 0, :], vecs[:, beta:beta + 1], None, ALU.mult)
                nc.vector.tensor_copy(mods[:, lv, GX, :], gate[:, lv, 1, :])
                nc.vector.tensor_copy(mods[:, lv, SA:SB + 1:SB - SA, :], raw[:, lv, 0:4:3, :])
                nc.vector.tensor_scalar(mods[:, lv, CA:CB + 1:CB - CA, :], raw[:, lv, 1:5:3, :], 1.0, None, ALU.add)


def block0(nc, g):
    ps, consts, vecs, mods, nhalf, xT, ident = (g[k] for k in ("ps", "consts", "vecs", "mods", "nhalf", "xT", "ident"))
    dve_passed, sp_passed = g["dve_passed"], g["sp_passed"]
    RING = 3
    PR = 3
    with ExitStack() as ctx:
        def sb(name, shape, dt=F32):
            return ctx.enter_context(nc.sbuf_tensor(name, shape, dt))

        def sem(name):
            return ctx.enter_context(nc.semaphore(name))

        wqkv = sb("wqkv", [P, 3, HEADS * DH])
        wout = sb("wout", [P, NC, D])
        gwi = sb("gwi", [P, FF0])
        gwo = sb("gwo", [P, FC, D])
        gbo = sb("gbo", [P, D])
        ewi = sb("ewi", [P, E, FF0])
        ewo = sb("ewo", [P, E, FC, D])
        ebo = sb("ebo", [E, D])
        bexp = sb("bexp", [P, (1 + E) * FC])
        brel = sb("brel", [P, (1 + E) * FC])
        mc = sb("mod_cur", [P, NM])
        tok = sb("tok", [P, NT, D])
        xcur = sb("xcur", [P, S])
        xg = sb("xg", [P, S])
        hcur = sb("hcur", [P, S])
        v = sb("v", [P, NT, HEADS * DH])
        hl = sb("hl", [P, 2, 4, S], F32R)
        stk = sb("stk", [P, RING, 2, HC, S], F32R)
        mcol = sb("mcol", [P, 2, HC * NT])
        mrow = sb("mrow", [HC * NT, 2, P], F32R)
        pr = sb("probs", [P, PR, HC, S])
        lnd = sb("lnd", [P, S])
        rden = sb("rden", [P, 2, S])
        oT = sb("oT", [P, NC, S])
        st6 = sb("st6", [P, NT, 6])
        mv = sb("mv", [P, NT, 2])
        ve = sb("ve", [P, NT])
        rs = sb("rs", [P, NT])
        hid = pr[:, 0:2]
        eb, rb = pr[:, 2, 0:2, :], pr[:, 2, 2:4, :]
        lgt = sb("lgt", [P, NT, D])
        mx8 = sb("mx8", [P, NT, 8])
        ix8 = sb("ix8", [P, NT, 8], U32)
        ixf = sb("ixf", [P, NT, 8])
        tv = sb("tv", [P, NT, 2])
        eq = sb("eq", [P, 2, NT, E])
        wt = sb("wt", [P, NT, E])
        wl = sb("wl", [P, NT, E])
        wT = sb("wT", [E, S])
        acc = sb("acc", [P, NT, D])

        w_in, w2_in, ones_set = sem("attention_weights_landed"), sem("expert_weights_landed"), sem("ones_set")
        bias_done = sem("bias_done")
        x_land, var_done, rstd_done, z_done = sem("x_landed"), sem("var_done"), sem("rstd_done"), sem("z_done")
        scr_full, drained = sem("scratch_full"), sem("scratch_drained")
        hi_done = sem("hi_done")
        stk_in = [sem(f"stack_landed_{i}") for i in range(RING)]
        m_in = [sem(f"max_landed_{i}") for i in range(2)]
        st_full, p_done, pv_done = sem("scores_full"), sem("probs_done"), sem("pv_done")
        rden_done, o_done, s_done = sem("rden_done"), sem("o_done"), sem("s_done")
        hid_full, e_done, r_done, h_done = sem("hidden_full"), sem("exp_done"), sem("relu_done"), sem("hidden_done")
        y_full, acc_done, lg_done, wt_done = sem("expert_out_full"), sem("acc_done"), sem("logits_done"), sem("gates_done")
        x2_done, fin_done = sem("x2_done"), sem("x_done")
        dch, ach = sem("dve_chain"), sem("act_chain")

        order = ["xT", "zT"] + [("v", t, h) for t in range(NT) for h in range(2)]
        order += [("q", 0), ("k", 0), ("q", 1), ("k", 1)] + [("mx", 0, i) for i in range(16)] + [("mT", 0)]
        slots = {}
        for c in range(NC):
            for kt in range(NT):
                u = []
                if kt == 0 and c + 2 < NC:
                    u += [("q", c + 2), ("k", c + 2)]
                if c + 1 < NC:
                    u += [("mx", c + 1, i) for i in (range(0, 5), range(5, 11), range(11, 16), [])[kt]]
                    if kt == 3:
                        u += [("mT", c + 1)]
                slots[c, kt] = u
                order += u
        order += ["o", "sT", "zB", "x2T", "zC", "lg", "wT", "bw", "aT"]
        use = {u: i for i, u in enumerate(order)}
        NU = len(order)
        NST = NC * NT
        NSL = [len(range(i, NC, RING)) for i in range(RING)]
        LAND = 3 * HC * 16
        NDCH, NACH = DVE_CHAIN, ACT_CHAIN
        NH = (1 + E) * FC

        def bank(u):
            return 4 + use[u] % 2

        block = ctx.enter_context(nc.Block())

        def max_row(sp, b, c):
            sp.wait_ge(drained, b * NU + use["mT", c] + 1)
            sp.sem_inc(sp_passed, 1)
            sp.dma_start(stk[96:97, c % RING, 0, :, :].rearrange("p j (t n) -> p (j t) n", n=P).bitcast(F32),
                         mrow[:, c % 2, :].bitcast(F32)).then_inc(m_in[c % 2], 16)

        @block.sync
        def _(sp):
            sp.dma_start(wqkv[:], g["wqkv_in"]).then_inc(w_in, 16)
            sp.dma_start(wout[:], g["wout_in"]).then_inc(w_in, 16)
            for dst, src in ((gwi, "gwi_in"), (gwo, "gwo_in"), (gbo, "gbo_in"), (ewi, "ewi_in"), (ewo, "ewo_in"), (ebo, "ebo_in")):
                sp.dma_start(dst[:], g[src].partition_broadcast(P) if dst is gbo else g[src]).then_inc(w2_in, 16)
            with sp.Fori(0, B) as b:
                sp.wait_ge(fin_done, b + 1)
                sp.sem_inc(sp_passed, 1)
                sp.dma_start(tok[:], g["x_tok"][b]).then_inc(x_land, 16)
                for c in range(NC):
                    sl, par = c % RING, c % 2
                    sp.wait_ge(drained, b * NU + use["k", c] + 1)
                    sp.sem_inc(sp_passed, 1)
                    if c >= RING:
                        sp.wait_ge(st_full, b * 2 * NST + 2 * NT * (c - RING + 1))
                        sp.sem_inc(sp_passed, 1)
                    for j in range(HC):
                        rows = slice(DH * j, DH * j + DH)
                        for r, (qs, ks) in enumerate(((0, 2), (1, 2), (0, 3))):
                            sp.dma_start(stk[DH * r:DH * r + DH, sl, :, j, :].bitcast(F32),
                                         hl[rows, par, qs:ks + 1:ks - qs, :].bitcast(F32)).then_inc(stk_in[sl], 16)
                    if c >= 1:
                        max_row(sp, b, c - 1)
                max_row(sp, b, NC - 1)

        @block.gpsimd
        def _(pool):
            with pool.Fori(0, B) as b:
                for k in range(3):
                    pool.wait_ge(var_done, 3 * b + k + 1)
                    nc.gpsimd.tensor_tensor(rs[:], ve[:], nhalf[:], ALU.pow).then_inc(rstd_done, 1)

        @block.tensor
        def _(pe):
            pe.wait_ge(w_in, 32)
            pe.wait_ge(ones_set, 1)
            with pe.Fori(0, B) as b:
                def scratch(u):
                    if use[u] >= 2:
                        pe.wait_ge(drained, b * NU + use[u] - 1)
                    return ps[:, bank(u), :]

                def turn(u, src, n=P):
                    to = scratch(u)
                    for t in range(NT):
                        mm = nc.tensor.transpose(to[:, t * P:(t + 1) * P], src(t), ident)
                    mm.then_inc(scr_full, 1)

                def project(c):
                    for w, nm in ((0, "q"), (1, "k")):
                        to = scratch((nm, c))
                        nc.tensor.matmul(to, wqkv[:, w, c * P:(c + 1) * P], hcur[:], start=True, stop=True).then_inc(scr_full, 1)

                def max_scores(c, i):
                    j, qt = i // NT, i % NT
                    to = scratch(("mx", c, i))
                    if i == 0:
                        pe.wait_ge(stk_in[c % RING], b * LAND * NSL[c % RING] + LAND * (c // RING + 1))
                    nc.tensor.matmul(to, stk[0:96, c % RING, 0, j, qt * P:(qt + 1) * P], stk[0:96, c % RING, 1, j, :],
                                     start=True, stop=True).then_inc(scr_full, 1)

                def max_turn(c):
                    to = scratch(("mT", c))
                    pe.wait_ge(drained, b * NU + use["mx", c, 15] + 1)
                    nc.tensor.transpose(to[0:HC * NT, 0:P], mcol[:, c % 2, :], ident).then_inc(scr_full, 1)

                def scores(c, kt, half):
                    n = (c * NT + kt) * 2 + half
                    if n >= 2:
                        pe.wait_ge(p_done, b * 2 * NST + n - 1)
                    if kt == 0 and half == 0:
                        pe.wait_ge(m_in[c % 2], 16 * (b * (NC // 2) + c // 2 + 1))
                    for jj in range(2):
                        j = 2 * half + jj
                        mm = nc.tensor.matmul(ps[:, 2 * half + jj, :], stk[0:97, c % RING, 1, j, kt * P:(kt + 1) * P],
                                              stk[0:97, c % RING, 0, j, :], start=True, stop=True)
                    mm.then_inc(st_full, 1)

                def values(n, what):
                    c, kt = n // NT, n % NT
                    if what == "v":
                        pe.wait_ge(p_done, b * 2 * NST + 2 * n + 2)
                        if kt == 0 and c:
                            pe.wait_ge(o_done, b * NC + c)
                    for j in range(HC):
                        h = HC * c + j
                        w, to = (v[:, kt, h * DH:(h + 1) * DH], 6) if what == "v" else (consts[:, ONES:ONES + DH], 7)
                        mm = nc.tensor.matmul(ps[DH * j:DH * j + DH, to, :], w, pr[:, n % PR, j, :],
                                              start=(kt == 0), stop=(kt == NT - 1), tile_position=(0, DH * j))
                    if what == "d":
                        mm.then_inc(pv_done, 1)

                pe.wait_ge(x_land, 16 * (b + 1))
                turn("xT", lambda t: tok[:, t, :])
                pe.wait_ge(z_done, 3 * b + 1)
                turn("zT", lambda t: tok[:, t, :])
                pe.wait_ge(drained, b * NU + use["zT"] + 1)
                for t in range(NT):
                    for h in range(2):
                        nc.tensor.matmul(scratch(("v", t, h)), hcur[:, t * P:(t + 1) * P], wqkv[:, 2, h * 512:(h + 1) * 512],
                                         start=True, stop=True).then_inc(scr_full, 1)
                project(0)
                project(1)
                for i in range(16):
                    max_scores(0, i)
                max_turn(0)
                for c in range(NC):
                    for kt in range(NT):
                        n = c * NT + kt
                        todo = [u for u in slots[c, kt] if u[0] == "mx"]

                        def some(k):
                            for u in todo[:k]:
                                max_scores(u[1], u[2])
                            del todo[:k]

                        scores(c, kt, 0)
                        if kt == 0 and c + 2 < NC:
                            project(c + 2)
                        some(1)
                        scores(c, kt, 1)
                        if kt == NT - 1 and c + 1 < NC:
                            max_turn(c + 1)
                        some(1)
                        if n:
                            values(n - 1, "v")
                            some(2)
                            values(n - 1, "d")
                        some(len(todo))
                values(NST - 1, "v")
                values(NST - 1, "d")
                pe.wait_ge(o_done, b * NC + NC)
                to = scratch("o")
                for c in range(NC):
                    mm = nc.tensor.matmul(to, wout[:, c, :], oT[:, c, :], start=(c == 0), stop=(c == NC - 1))
                mm.then_inc(scr_full, 1)
                pe.wait_ge(drained, b * NU + use["o"] + 1)
                turn("sT", lambda t: xg[:, t * P:(t + 1) * P])
                pe.wait_ge(z_done, 3 * b + 2)
                turn("zB", lambda t: tok[:, t, :])
                pe.wait_ge(drained, b * NU + use["zB"] + 1)
                turn("x2T", lambda t: xcur[:, t * P:(t + 1) * P])
                pe.wait_ge(z_done, 3 * b + 3)
                turn("zC", lambda t: tok[:, t, :])
                pe.wait_ge(drained, b * NU + use["zC"] + 1)
                pe.wait_ge(w2_in, 16 * 6)

                def hidden(n):
                    for f in range(FC):
                        k = n * FC + f
                        if k >= 4:
                            pe.wait_ge(h_done, b * NH + k - 3)
                        w = gwi[:, f * P:(f + 1) * P] if n == 0 else ewi[:, n - 1, f * P:(f + 1) * P]
                        nc.tensor.matmul(ps[:, k % 4, :], w, hcur[:], start=True, stop=True).then_inc(hid_full, 1)

                def expert_out(n):
                    pe.wait_ge(h_done, b * NH + n * FC + FC)
                    if n >= 3:
                        pe.wait_ge(acc_done, b * E + n - 2)
                    for t in range(NT):
                        for f in range(FC):
                            mm = nc.tensor.matmul(ps[:, 6 + n % 2, t * P:(t + 1) * P], hid[:, n % 2, f, t * P:(t + 1) * P],
                                                  ewo[:, n - 1, f, :], start=(f == 0), stop=(f == FC - 1))
                    mm.then_inc(y_full, 1)

                hidden(0)
                pe.wait_ge(h_done, b * NH + FC)
                to = scratch("lg")
                for t in range(NT):
                    for f in range(FC):
                        mm = nc.tensor.matmul(to[:, t * P:(t + 1) * P], hid[:, 0, f, t * P:(t + 1) * P], gwo[:, f, :],
                                              start=(f == 0), stop=(f == FC - 1))
                mm.then_inc(scr_full, 1)
                hidden(1)
                hidden(2)
                pe.wait_ge(wt_done, b + 1)
                to = scratch("wT")
                for t in range(NT):
                    mm = nc.tensor.transpose(to[0:E, t * P:(t + 1) * P], wt[:, t, :], ident)
                mm.then_inc(scr_full, 1)
                pe.wait_ge(drained, b * NU + use["wT"] + 1)
                to = scratch("bw")
                for t in range(NT):
                    mm = nc.tensor.matmul(to[:, t * P:(t + 1) * P], wT[:, t * P:(t + 1) * P], ebo[:], start=True, stop=True)
                mm.then_inc(scr_full, 1)
                expert_out(1)
                for n in range(3, 1 + E):
                    hidden(n)
                    expert_out(n - 1)
                expert_out(E)
                pe.wait_ge(acc_done, b * E + E)
                turn("aT", lambda t: acc[:, t, :])

        @block.scalar
        def _(act):
            nc.scalar.preload_act_table_set("natural_log_exp_and_others")
            with act.Fori(0, B) as b:
                k = [0]

                def high(c):
                    par = c % 2
                    if c >= 2:
                        act.wait_ge(stk_in[(c - 2) % RING], b * LAND * NSL[(c - 2) % RING] + LAND * ((c - 2) // RING + 1))
                    for nm, at in (("q", 0), ("k", 2)):
                        act.wait_ge(scr_full, b * NU + use[nm, c] + 1)
                        nc.scalar.activation(hl[:, par, at, :], ps[:, bank((nm, c)), :], ACT.Identity).then_inc(hi_done, 1)

                def inverse(c):
                    act.wait_ge(pv_done, b * NST + NT * c + NT)
                    k[0] += 1
                    nc.scalar.activation(lnd[:], ps[:, 7, :], ACT.Ln).then_inc(ach, 1)
                    act.wait_ge(ach, b * NACH + k[0])
                    if c >= 2:
                        act.wait_ge(o_done, b * NC + c - 1)
                    nc.scalar.activation(rden[:, c % 2, :], lnd[:], ACT.Exp, scale=-1.0).then_inc(rden_done, 1)

                high(0)
                high(1)
                for c in range(NC):
                    for kt in range(NT):
                        n = c * NT + kt
                        if n >= PR:
                            act.wait_ge(pv_done, b * NST + n - PR + 1)
                        for half in range(2):
                            act.wait_ge(st_full, b * 2 * NST + 2 * n + half + 1)
                            nc.scalar.activation(pr[:, n % PR, 2 * half:2 * half + 2, :], ps[:, 2 * half:2 * half + 2, :],
                                                 ACT.Exp, scale=SCALE).then_inc(p_done, 1)
                            if half == 0 and kt == 0 and c + 2 < NC:
                                high(c + 2)
                        if kt == 0 and c >= 1:
                            inverse(c - 1)
                inverse(NC - 1)
                assert k[0] == NACH, k
                for n in range(1 + E):
                    for f in range(FC):
                        i = n * FC + f
                        act.wait_ge(hid_full, b * NH + i + 1)
                        if i >= 2:
                            act.wait_ge(h_done, b * NH + i - 1)
                        nc.scalar.activation(eb[:, i % 2, :], ps[:, i % 4, :], ACT.Exp, bias=bexp[:, i:i + 1]).then_inc(e_done, 1)

        @block.vector
        def _(dve):
            dve.sem_inc(fin_done, 1)
            nc.vector.memset(stk[96:97, :, 1, :, :].bitcast(F32), 1.0).then_inc(ones_set, 1)
            nc.vector.tensor_scalar(bexp[:], vecs[:, GBI:GBI + NH], float(np.log(SELU_A)), None, ALU.add).then_inc(bias_done, 1)
            nc.vector.tensor_scalar(brel[:], vecs[:, GBI:GBI + NH], -SELU_A, None, ALU.add).then_inc(bias_done, 1)
            dve.wait_ge(bias_done, 2)
            with dve.Fori(0, B) as b:
                k = [0]

                def then(ins):
                    k[0] += 1
                    ins.then_inc(dch, 1)
                    dve.wait_ge(dch, b * NDCH + k[0])

                def full(u):
                    dve.wait_ge(scr_full, b * NU + use[u] + 1)
                    return ps[:, bank(u), :]

                def normalise(i, src, eps, free):
                    for t in range(NT):
                        ins = nc.vector.bn_stats(st6[:, t, :], src(t))
                    then(ins)
                    dve.sem_inc(dve_passed, 1)
                    for t in range(NT):
                        ins = nc.vector.bn_aggr(mv[:, t, :], st6[:, t, :])
                    then(ins)
                    nc.vector.tensor_scalar(ve[:], mv[:, :, 1], eps, None, ALU.add).then_inc(var_done, 1)
                    dve.wait_ge(rstd_done, 3 * b + i + 1)
                    for t in range(NT):
                        ins = nc.vector.tensor_scalar(tok[:, t, :], src(t), mv[:, t, 0:1], rs[:, t:t + 1], ALU.subtract, ALU.mult)
                    ins.then_inc(z_done, 1)
                    if free:
                        dve.wait_ge(z_done, 3 * b + i + 1)
                        nc.vector.tensor_copy(ve[:], mv[:, :, 1]).then_inc(drained, 1)

                then(nc.vector.tensor_copy(mc[:], mods[:, 0, :, bass.ds(b, 1)].rearrange("p m o -> p (m o)")))
                nc.vector.tensor_copy(xcur[:], full("xT")).then_inc(drained, 1)
                normalise(0, lambda t: tok[:, t, :], 1e-5, False)
                nc.vector.tensor_scalar(hcur[:], full("zT"), mc[:, CA:CA + 1], mc[:, SA:SA + 1], ALU.mult, ALU.add).then_inc(drained, 1)
                for t in range(NT):
                    for h in range(2):
                        nc.vector.tensor_copy(v[:, t, h * 512:(h + 1) * 512], full(("v", t, h))).then_inc(drained, 1)

                def drain(u):
                    if u[0] in "qk":
                        c, at = u[1], 0 if u[0] == "q" else 2
                        src = full(u)
                        dve.wait_ge(hi_done, 2 * (b * NC + c) + at // 2 + 1)
                        nc.vector.tensor_tensor(hl[:, c % 2, at + 1, :], src, hl[:, c % 2, at, :].bitcast(F32),
                                                ALU.subtract).then_inc(drained, 1)
                    elif u[0] == "mx":
                        c, i = u[1], u[2]
                        nc.vector.tensor_reduce(mcol[:, c % 2, i:i + 1], full(u), AX, ALU.max).then_inc(drained, 1)
                    else:
                        c = u[1]
                        src = full(u)
                        if c >= 2:
                            dve.wait_ge(m_in[c % 2], 16 * (b * (NC // 2) + c // 2))
                        nc.vector.tensor_scalar(mrow[:, c % 2, :], src[0:HC * NT, 0:P], -1.0, None, ALU.mult).then_inc(drained, 1)

                def attended(c):
                    dve.wait_ge(rden_done, b * NC + c + 1)
                    nc.vector.tensor_tensor(oT[:, c, :], ps[:, 6, :], rden[:, c % 2, :], ALU.mult).then_inc(o_done, 1)

                for u in order[use["q", 0]:use["mT", 0] + 1]:
                    drain(u)
                for c in range(NC):
                    for kt in range(NT):
                        for u in slots[c, kt]:
                            drain(u)
                        if kt == 0 and c >= 1:
                            attended(c - 1)
                attended(NC - 1)
                nc.vector.tensor_scalar(xg[:], full("o"), vecs[:, BO0:BO0 + 1], None, ALU.add).then_inc(drained, 1)
                src = full("sT")
                normalise(1, lambda t: src[:, t * P:(t + 1) * P], 1e-6, True)
                src = full("zB")
                then(nc.vector.tensor_scalar(xg[:], xcur[:], mc[:, GB:GB + 1], None, ALU.add))
                nc.vector.scalar_tensor_tensor(xcur[:], src, mc[:, GG:GG + 1], xg[:], ALU.mult, ALU.add).then_inc(drained, 1)
                src = full("x2T")
                normalise(2, lambda t: src[:, t * P:(t + 1) * P], 1e-5, True)
                nc.vector.tensor_scalar(hcur[:], full("zC"), mc[:, CB:CB + 1], mc[:, SB:SB + 1], ALU.mult, ALU.add).then_inc(drained, 1)

                def selu(n):
                    if n >= 2:
                        if n > 2:
                            dve.wait_ge(y_full, b * E + n - 2)
                    for f in range(FC):
                        i = n * FC + f
                        dve.wait_ge(e_done, b * NH + i + 1)
                        nc.vector.tensor_scalar(rb[:, i % 2, :], ps[:, i % 4, :], brel[:, i:i + 1], -SELU_A,
                                                ALU.add, ALU.max).then_inc(r_done, 1)
                        dve.wait_ge(r_done, b * NH + i + 1)
                        nc.vector.scalar_tensor_tensor(hid[:, n % 2, f, :], eb[:, i % 2, :], SELU_A, rb[:, i % 2, :],
                                                       ALU.min, ALU.add).then_inc(h_done, 1)

                def accumulate(n):
                    dve.wait_ge(y_full, b * E + n)
                    for t in range(NT):
                        ins = nc.vector.scalar_tensor_tensor(acc[:, t, :], ps[:, 6 + n % 2, t * P:(t + 1) * P],
                                                             wl[:, t, n - 1:n], acc[:, t, :], ALU.mult, ALU.add)
                    ins.then_inc(acc_done, 1)
                    dve.wait_ge(acc_done, b * E + n)

                selu(0)
                nc.vector.scalar_tensor_tensor(lgt[:], full("lg").rearrange("p (t d) -> p t d", d=D), SELU_L,
                                               gbo[:].unsqueeze(1).to_broadcast([P, NT, D]), ALU.mult, ALU.add).then_inc(drained, 1)
                selu(1)
                dve.wait_ge(drained, b * NU + use["lg"] + 1)
                dve.sem_inc(dve_passed, 1)
                for t in range(NT):
                    ins = nc.vector.max(mx8[:, t, :], lgt[:, t, :])
                then(ins)
                dve.sem_inc(dve_passed, 1)
                for t in range(NT):
                    ins = nc.vector.max_index(ix8[:, t, :], mx8[:, t, :], lgt[:, t, :])
                nc.vector.tensor_tensor(ve[:], mx8[:, :, 0], mx8[:, :, 1], ALU.add)
                then(ins)
                then(nc.vector.tensor_copy(ixf[:], ix8[:]))
                then(nc.vector.reciprocal(rs[:], ve[:]))
                then(nc.vector.tensor_tensor(tv[:], mx8[:, :, 0:2], rs[:].unsqueeze(2).to_broadcast([P, NT, 2]), ALU.mult))
                iota = consts[:, IOTA:IOTA + E].unsqueeze(1).to_broadcast([P, NT, E])
                for i in range(2):
                    ins = nc.vector.tensor_tensor(eq[:, i], iota, ixf[:, :, i:i + 1].to_broadcast([P, NT, E]), ALU.is_equal)
                then(ins)
                for i in range(2):
                    ins = nc.vector.tensor_tensor(eq[:, i], eq[:, i], tv[:, :, i:i + 1].to_broadcast([P, NT, E]), ALU.mult)
                then(ins)
                then(nc.vector.tensor_tensor(wt[:], eq[:, 0], eq[:, 1], ALU.add))
                nc.vector.tensor_scalar(wl[:], wt[:], SELU_L, None, ALU.mult).then_inc(wt_done, 1)
                selu(2)
                nc.vector.tensor_copy(wT[:], full("wT")[0:E, :]).then_inc(drained, 1)
                nc.vector.tensor_copy(acc[:].rearrange("p t d -> p (t d)"), full("bw")).then_inc(drained, 1)
                dve.wait_ge(drained, b * NU + use["bw"] + 1)
                accumulate(1)
                for n in range(3, 1 + E):
                    selu(n)
                    accumulate(n - 1)
                accumulate(E)
                nc.vector.scalar_tensor_tensor(xT[:, bass.ds(b, 1), :].rearrange("p o s -> p (o s)"), full("aT"), mc[:, GX:GX + 1],
                                               xcur[:], ALU.mult, ALU.add).then_inc(drained, 1)
                dve.wait_ge(drained, b * NU + NU)
                nc.vector.tensor_copy(ve[:], mv[:, :, 1]).then_inc(fin_done, 1)
                assert k[0] == NDCH, k


DVE_CHAIN = 16
ACT_CHAIN = NC


def layers(nc, g):
    ps, consts, vecs, mods, nhalf, xT, ident = (g[k] for k in ("ps", "consts", "vecs", "mods", "nhalf", "xT", "ident"))
    LNS = ("in", "1", "2", "out")
    with ExitStack() as ctx:
        def sb(name, shape, dt=F32):
            return ctx.enter_context(nc.sbuf_tensor(name, shape, dt))

        def sem(name):
            return ctx.enter_context(nc.semaphore(name))

        w = sb("layer_w", [P, 2, LW])
        bkv = sb("layer_bkv", [P, 2, 2 * D])
        bq1 = sb("bq1", [P, 2])
        h = sb("h", [P, B, S])
        s = sb("s", [P, B, S])
        z = sb("z", [P, B, NT, D])
        ex = sb("ex", [P, B, S])
        q = sb("q", [P, B, S])
        kv = sb("kv", [P, B, NT, 2 * D + 1])
        kf = sb("kf", [P, B, NT, D])
        kvm = sb("kvm", [P, B, D + LH])
        dn = sb("dn", [P, B, NT, LH])
        hid = sb("layer_hid", [P, B, LFC, S])
        st6 = sb("l_st6", [P, B, NT, 6])
        mv = sb("l_mv", [P, B, NT, 2])
        ve = sb("l_ve", [P, B, 2, NT])
        rs = sb("l_rs", [P, B, NT])
        nm = sb("l_nm", [P, B, NT])
        xg = sb("l_xg", [P, B, S])

        w_in = [sem(f"layer_w_landed_{i}") for i in range(2)]
        names = ("q_full q_exp q_clip q_done kv_full kv_done k_exp k_clip k_done kvs_full kvm_done att_full den_done "
                 "rec_done at_done atT_full atT_done o_full o_sum fa_full fa_done fb_full fb_done y_full y_sum bq1_done one_set").split()
        S_ = {k: sem(k) for k in names}
        ln = {k: {x: sem(f"ln_{k}_{x}") for x in ("full", "stats", "aggr", "var", "rs", "rstd", "z", "zfull", "done") if (k, x) != ("in", "done")} for k in LNS}
        ln["in"]["done"] = ln["2"]["done"]
        xg_done = sem("xg_done")
        w_free = sem("layer_w_free")

        FIRST, SECOND = (0, 1), (2, 3)
        A1, A2 = ("q", "kv"), ("kvs", "att", "atT", "o", "sT1", "zT1")
        M1, M2 = ("w1a", "w1b"), ("y", "sT2", "zT2")

        def merge(*lists):
            n = max(len(x) for x in lists)
            keyed = [((i + 0.5) * n / len(x), j, u) for j, x in enumerate(lists) for i, u in enumerate(x)]
            return [u for _, _, u in sorted(keyed, key=lambda t: t[:2])]

        def chain(stages, pair, l, par):
            return [(st, e, l, par) for st in stages for e in pair]

        def layer(l, par, prev=None):
            first = merge(chain(A1, FIRST, l, par), chain(M2, SECOND, prev, 1 - par)) if prev is not None else chain(A1, FIRST, l, par)
            return (first + merge(chain(A2, FIRST, l, par), chain(A1, SECOND, l, par))
                    + merge(chain(M1, FIRST, l, par), chain(A2, SECOND, l, par))
                    + merge(chain(M2, FIRST, l, par), chain(M1, SECOND, l, par)))

        def run(eng, part, late=None):
            def go(stages):
                before = None
                for u in stages:
                    part(*u)
                    if late and before:
                        late(*before)
                    before = u
                if late:
                    late(*before)

            go([("sTin", e, 0, 0) for e in range(B)] + [("zTin", e, 0, 0) for e in range(B)])
            go(layer(0, 0))
            with eng.Fori(0, LAYERS // 2 - 1) as i:
                for k in (1, 2):
                    go(layer(i * 2 + k, k % 2, i * 2 + (k - 1)))
            go(layer(LAYERS - 1, 1, LAYERS - 2) + chain(M2, SECOND, LAYERS - 1, 1))
            go([("sTout", e, 0, 0) for e in range(B)] + [("zTout", e, 0, 0) for e in range(B)])

        def at(l, e, n=1, k=0):
            return (l * B + e) * n + k + 1

        def which(st):
            return {"sTin": "in", "sT1": "1", "sT2": "2", "sTout": "out"}[st]

        block = ctx.enter_context(nc.Block())

        @block.sync
        def _(sp):
            def load(l, par):
                sp.dma_start(w[:, par, :], g["lw_in"][l]).then_inc(w_in[par], 16)
                sp.dma_start(bkv[:, par, :], g["bkv_in"][l].partition_broadcast(P)).then_inc(w_in[par], 16)

            load(0, 0)
            load(1, 1)
            sp.dma_start(g["rw"][:], g["rw_in"]).then_inc(g["w1_in"], 16)
            sp.dma_start(g["gu"][:], g["gu_in"]).then_inc(g["w1_in"], 16)
            for k, (a, n) in enumerate(FCH):
                sp.dma_start(g["dn1"][0:n, k, :, :], g["dn_in"][a:a + n]).then_inc(g["w1_in"], 16)
            with sp.Fori(0, LAYERS // 2 - 1) as i:
                for par in range(2):
                    sp.wait_ge(w_free, i * 2 + par + 1)
                    sp.sem_inc(g["sp_passed"], 1)
                    load(i * 2 + par + 2, par)

        @block.tensor
        def _(pe):
            pe.wait_ge(S_["one_set"], 1)

            def part(st, e, l, par):
                A, Bk = ps[:, 2 * e, :], ps[:, 2 * e + 1, :]
                W = w[:, par, :]
                if st == "q":
                    if e == 0:
                        pe.wait_ge(w_in[par], (l - par) * 16 + 32)
                    pe.wait_ge(ln["2"]["done"], at(l, e))
                    nc.tensor.matmul(A, W[:, WQ:WQ + D], h[:, e, :], start=True, stop=True).then_inc(S_["q_full"], 1)
                elif st == "kv":
                    for i, bk in enumerate((Bk, A)):
                        if i == 1:
                            pe.wait_ge(S_["q_done"], at(l, e))
                        for t in range(2):
                            mm = nc.tensor.matmul(bk[:, t * 2 * D:(t + 1) * 2 * D], h[:, e, (2 * i + t) * P:(2 * i + t + 1) * P],
                                                  W[:, WKV:WKV + 2 * D], start=True, stop=True)
                        mm.then_inc(S_["kv_full"], 1)
                elif st == "kvs":
                    pe.wait_ge(S_["k_done"], at(l, e))
                    for t in range(NT):
                        mm = nc.tensor.matmul(Bk[:, 0:D + 1], kf[:, e, t, :], kv[:, e, t, D:2 * D + 1], start=(t == 0), stop=(t == NT - 1))
                    mm.then_inc(S_["kvs_full"], 1)
                elif st == "att":
                    pe.wait_ge(S_["kvm_done"], at(l, e, 2, 1))
                    for t in range(NT):
                        bk = (A, Bk)[t // 2]
                        mm = nc.tensor.matmul(bk[:, (t % 2) * (D + LH):(t % 2 + 1) * (D + LH)], q[:, e, t * P:(t + 1) * P], kvm[:, e, :],
                                              start=True, stop=True)
                    mm.then_inc(S_["att_full"], 1)
                elif st == "atT":
                    pe.wait_ge(S_["at_done"], at(l, e))
                    for t in range(NT):
                        mm = nc.tensor.transpose(A[:, t * P:(t + 1) * P], z[:, e, t, :], ident)
                    mm.then_inc(S_["atT_full"], 1)
                elif st == "o":
                    pe.wait_ge(S_["atT_done"], at(l, e))
                    nc.tensor.matmul(Bk, W[:, WO:WO + D], s[:, e, :], start=True, stop=True).then_inc(S_["o_full"], 1)
                elif st in ("w1a", "w1b"):
                    if st == "w1a":
                        pe.wait_ge(ln["1"]["done"], at(l, e))
                    k = int(st == "w1b")
                    for i, bk in enumerate((A, Bk)):
                        f = 2 * k + i
                        if k:
                            pe.wait_ge(S_["fa_done"], at(l, e, 2, i))
                        nc.tensor.matmul(bk, W[:, W1 + f * P:W1 + (f + 1) * P], h[:, e, :],
                                         start=True, stop=True).then_inc(S_[("fa_full", "fb_full")[k]], 1)
                elif st == "y":
                    pe.wait_ge(S_["fb_done"], at(l, e, 2, 1))
                    for f in range(LFC):
                        mm = nc.tensor.matmul(A, W[:, W2 + f * D:W2 + (f + 1) * D], hid[:, e, f, :], start=(f == 0), stop=(f == LFC - 1))
                    mm.then_inc(S_["y_full"], 1)
                elif st[:2] == "sT":
                    k = which(st)
                    if k == "1":
                        pe.wait_ge(S_["o_sum"], at(l, e))
                    elif k == "2":
                        pe.wait_ge(S_["y_sum"], at(l, e))
                    elif k == "out":
                        pe.wait_ge(ln["2"]["done"], at(LAYERS, e))
                    src = {"in": xT, "out": h}.get(k, s)
                    bk = {"1": A, "2": Bk, "in": Bk, "out": Bk}[k]
                    for t in range(NT):
                        mm = nc.tensor.transpose(bk[:, t * P:(t + 1) * P], src[:, e, t * P:(t + 1) * P], ident)
                    mm.then_inc(ln[k]["full"], 1)
                else:
                    k = st[2:]
                    pe.wait_ge(ln[k]["z"], at(l, e))
                    bk = {"1": Bk}.get(k, A)
                    for t in range(NT):
                        mm = nc.tensor.transpose(bk[:, t * P:(t + 1) * P], z[:, e, t, :], ident)
                    mm.then_inc(ln[k]["zfull"], 1)

            run(pe, part)

        @block.scalar
        def _(act):
            def part(st, e, l, par):
                A, Bk = ps[:, 2 * e, :], ps[:, 2 * e + 1, :]
                col = lambda k: w[:, par, k:k + 1]
                if st == "q":
                    act.wait_ge(S_["q_full"], at(l, e))
                    nc.scalar.activation(ex[:, e, :], A, ACT.Exp, bias=col(BQ)).then_inc(S_["q_exp"], 1)
                elif st == "kv":
                    act.wait_ge(S_["kv_done"], at(l, e, 2, 1))
                    nc.scalar.activation(ex[:, e, :].rearrange("p (t d) -> p t d", d=D), kv[:, e, :, 0:D], ACT.Exp).then_inc(S_["k_exp"], 1)
                elif st == "atT":
                    act.wait_ge(S_["atT_full"], at(l, e))
                    nc.scalar.activation(s[:, e, :], A, ACT.Identity).then_inc(S_["atT_done"], 1)
                elif st in ("w1a", "w1b"):
                    k, (full, done) = (0, ("fa_full", "fa_done")) if st == "w1a" else (1, ("fb_full", "fb_done"))
                    for i, bk in enumerate((A, Bk)):
                        f = 2 * k + i
                        act.wait_ge(S_[full], at(l, e, 2, i))
                        nc.scalar.activation(hid[:, e, f, :], bk, ACT.Gelu, bias=col(LC1 + f)).then_inc(S_[done], 1)
                elif st[:2] == "sT":
                    k = which(st)
                    bk = {"1": A}.get(k, Bk)
                    act.wait_ge(ln[k]["rstd"], at(l, e))
                    for t in range(NT):
                        ins = nc.scalar.activation(z[:, e, t, :], bk[:, t * P:(t + 1) * P], ACT.Identity,
                                                   bias=nm[:, e, t:t + 1], scale=rs[:, e, t:t + 1])
                    ins.then_inc(ln[k]["z"], 1)

            run(act, part)

        @block.gpsimd
        def _(pool):
            def part(st, e, l, par):
                if st in ("q", "kv"):
                    k = st[0]
                    pool.wait_ge(S_[k + "_exp"], at(l, e))
                    pool.sem_inc(g["pool_passed"], 1)
                    nc.gpsimd.tensor_scalar(ex[:, e, :], ex[:, e, :], 1.0, 0.0, ALU.min, ALU.max).then_inc(S_[k + "_clip"], 1)
                elif st[:2] == "sT":
                    k = which(st)
                    pool.wait_ge(ln[k]["var"], at(l, e))
                    nc.gpsimd.tensor_tensor(rs[:, e, :], ve[:, e, 0, :], nhalf[:], ALU.pow).then_inc(ln[k]["rs"], 1)
                    pool.wait_ge(ln[k]["rs"], at(l, e))
                    nc.gpsimd.tensor_tensor(nm[:, e, :], ve[:, e, 1, :], rs[:, e, :], ALU.mult).then_inc(ln[k]["rstd"], 1)

            run(pool, part)

        @block.vector
        def _(dve):
            nc.vector.memset(kv[:, :, :, 2 * D:2 * D + 1], 1.0).then_inc(S_["one_set"], 1)

            def part(st, e, l, par):
                A, Bk = ps[:, 2 * e, :], ps[:, 2 * e + 1, :]
                col = lambda k: w[:, par, k:k + 1]
                if st == "q" and e in (FIRST[0],):
                    dve.wait_ge(w_in[par], (l - par) * 16 + 32)
                    nc.vector.tensor_scalar(bq1[:, par:par + 1], col(BQ), 1.0, None, ALU.add).then_inc(S_["bq1_done"], 1)
                elif st == "kv":
                    for i, bk in enumerate((Bk, A)):
                        dve.wait_ge(S_["kv_full"], at(l, e, 2, i))
                        nc.vector.tensor_tensor(kv[:, e, 2 * i:2 * i + 2, 0:2 * D], bk.rearrange("p (t d) -> p t d", d=2 * D),
                                                bkv[:, par, :].unsqueeze(1).to_broadcast([P, 2, 2 * D]), ALU.add).then_inc(S_["kv_done"], 1)
                elif st == "kvs":
                    dve.wait_ge(S_["kvs_full"], at(l, e))
                    nc.vector.tensor_tensor(kvm[:, e, 0:D], Bk[:, 0:D], consts[:, BLOCKS:BLOCKS + D], ALU.mult).then_inc(S_["kvm_done"], 1)
                    nc.vector.tensor_scalar(kvm[:, e, D:D + LH], consts[:, HSEL:HSEL + LH], Bk[:, D:D + 1], None, ALU.mult).then_inc(S_["kvm_done"], 1)
                elif st == "att":
                    dve.wait_ge(S_["att_full"], at(l, e))
                    both = [bk[:, 0:2 * (D + LH)].rearrange("p (t n) -> p t n", n=D + LH) for bk in (A, Bk)]
                    for i in range(2):
                        ins = nc.vector.tensor_scalar(dn[:, e, 2 * i:2 * i + 2, :], both[i][:, :, D:D + LH], 1e-6, None, ALU.add)
                    ins.then_inc(S_["den_done"], 1)
                    dve.wait_ge(S_["den_done"], at(l, e))
                    nc.vector.reciprocal(dn[:, e], dn[:, e]).then_inc(S_["rec_done"], 1)
                    dve.wait_ge(S_["rec_done"], at(l, e))
                    for i in range(2):
                        ins = nc.vector.tensor_tensor(z[:, e, 2 * i:2 * i + 2, :].rearrange("p t (a c) -> p t a c", c=LD),
                                                      both[i][:, :, 0:D].rearrange("p t (a c) -> p t a c", c=LD),
                                                      dn[:, e, 2 * i:2 * i + 2, :].unsqueeze(3).to_broadcast([P, 2, LH, LD]), ALU.mult)
                    ins.then_inc(S_["at_done"], 1)
                elif st in ("o", "y"):
                    bk, bias = (Bk, LBO) if st == "o" else (A, LC2)
                    dve.wait_ge(S_[st + "_full"], at(l, e))
                    ins = nc.vector.scalar_tensor_tensor(s[:, e, :], bk, col(bias), h[:, e, :], ALU.add, ALU.add)
                    ins.then_inc(S_[st + "_sum"], 1)
                elif st[:2] == "sT":
                    k = which(st)
                    bk = {"1": A}.get(k, Bk)
                    dve.wait_ge(ln[k]["full"], at(l, e))
                    for t in range(NT):
                        ins = nc.vector.bn_stats(st6[:, e, t, :], bk[:, t * P:(t + 1) * P])
                    ins.then_inc(ln[k]["stats"], 1)
                    dve.wait_ge(ln[k]["stats"], at(l, e))
                    dve.sem_inc(g["dve_passed"], 1)
                    for t in range(NT):
                        ins = nc.vector.bn_aggr(mv[:, e, t, :], st6[:, e, t, :])
                    ins.then_inc(ln[k]["aggr"], 1)
                    dve.wait_ge(ln[k]["aggr"], at(l, e))
                    nc.vector.tensor_scalar(ve[:, e, 1, :], mv[:, e, :, 0], -1.0, None, ALU.mult)
                    nc.vector.tensor_scalar(ve[:, e, 0, :], mv[:, e, :, 1], 1e-5, None, ALU.add).then_inc(ln[k]["var"], 1)
                elif st[:2] == "zT":
                    k = st[2:]
                    bk = {"1": Bk}.get(k, A)
                    dve.wait_ge(ln[k]["zfull"], at(l, e))
                    if k == "out":
                        nc.vector.tensor_scalar(xg[:, e, :], xT[:, e, :], mods[:, 1, GB, e:e + 1], None, ALU.add).then_inc(xg_done, 1)
                        dve.wait_ge(xg_done, e + 1)
                        ins = nc.vector.scalar_tensor_tensor(xT[:, e, :], bk, mods[:, 1, GG, e:e + 1], xg[:, e, :], ALU.mult, ALU.add)
                    else:
                        a, c = {"in": (mods[:, 1, CA, e:e + 1], mods[:, 1, SA, e:e + 1]), "1": (col(LG1), col(LBE1)),
                                "2": (col(LG2), col(LBE2))}[k]
                        ins = nc.vector.tensor_scalar(h[:, e, :], bk, a, c, ALU.mult, ALU.add)
                    ins.then_inc(ln[k]["done"], 1)
                    if k == "2" and e == B - 1:
                        dve.wait_ge(ln[k]["done"], at(l + 1, e))
                        nc.vector.tensor_copy(dn[:, e, 0, 0:1], dn[:, e, 0, 1:2]).then_inc(w_free, 1)

            def late(st, e, l, par):
                A = ps[:, 2 * e, :]
                if st == "q":
                    dve.wait_ge(S_["bq1_done"], l + 1)
                    dve.wait_ge(S_["q_clip"], at(l, e))
                    nc.vector.scalar_tensor_tensor(q[:, e, :], A, bq1[:, par:par + 1], ex[:, e, :], ALU.add, ALU.max).then_inc(S_["q_done"], 1)
                elif st == "kv":
                    dve.wait_ge(S_["k_clip"], at(l, e))
                    nc.vector.scalar_tensor_tensor(kf[:, e], kv[:, e, :, 0:D], 1.0, ex[:, e, :].rearrange("p (t d) -> p t d", d=D),
                                                   ALU.add, ALU.max).then_inc(S_["k_done"], 1)

            run(dve, part, late)


def experts1(nc, g):
    ps, consts, vecs, mods, nhalf, xT, ident = (g[k] for k in ("ps", "consts", "vecs", "mods", "nhalf", "xT", "ident"))
    rw, gu, dn1, w1_in = (g[k] for k in ("rw", "gu", "dn1", "w1_in"))
    KF = len(FCH)
    with ExitStack() as ctx:
        def sb(name, shape, dt=F32):
            return ctx.enter_context(nc.sbuf_tensor(name, shape, dt))

        def sem(name):
            return ctx.enter_context(nc.semaphore(name))

        mc = sb("m_cur", [P, NM])
        xcur = sb("e_x", [P, S])
        hcur = sb("e_h", [P, S])
        z = sb("e_z", [P, NT, D])
        st6, mv, ve, rs = sb("e_st6", [P, NT, 6]), sb("e_mv", [P, NT, 2]), sb("e_ve", [P, NT]), sb("e_rs", [P, NT])
        sg = sb("e_silu", [P, 2, S])
        hid = sb("e_hid", [P, 2, KF, S])
        acc = sb("e_acc", [P, NT, D])
        outb = sb("e_out", [P, NT, D])
        fin = sb("e_fin", [P, S])
        pb = sb("e_probs", [P, NT, E])
        mx8 = sb("e_mx8", [P, NT, 8])
        ix8 = sb("e_ix8", [P, NT, 8], U32)
        ixf = sb("e_ixf", [P, NT, 8])
        tv = sb("e_tv", [P, NT, 2])
        eq = sb("e_eq", [P, 2, NT, E])
        wt = sb("e_wt", [P, NT, E])

        scr_full, drained = sem("e_scratch_full"), sem("e_scratch_drained")
        var_done, rstd_done, z_done = sem("e_var"), sem("e_rstd"), sem("e_z")
        g_full, u_full, s_done, h_done = sem("g_full"), sem("u_full"), sem("silu_done1"), sem("hid_done1")
        y_full, acc_done = sem("y_full1"), sem("acc_done1")
        m_done, pe_done = sem("router_max"), sem("router_exp")
        out_done, stored, dch = sem("out_done"), sem("stored"), sem("e_chain")
        x_done = sem("e_x_done")

        order = ["xT", "zT", "rt", "aT", "fT"]
        use = {u: i for i, u in enumerate(order)}
        NU, NH, NDCH = len(order), U * KF, DVE_CHAIN1

        def bank(u):
            return 4 + use[u] % 2

        block = ctx.enter_context(nc.Block())

        @block.sync
        def _(sp):
            sp.sem_inc(stored, 16)
            with sp.Fori(0, B) as b:
                sp.wait_ge(out_done, b + 1)
                sp.sem_inc(g["sp_passed"], 1)
                sp.dma_start(g["out_tok"][b], outb[:]).then_inc(stored, 16)
            sp.wait_ge(stored, 16 * (B + 1))

        @block.gpsimd
        def _(pool):
            with pool.Fori(0, B) as b:
                pool.wait_ge(var_done, b + 1)
                nc.gpsimd.tensor_tensor(rs[:], ve[:], nhalf[:], ALU.pow).then_inc(rstd_done, 1)

        @block.tensor
        def _(pe):
            pe.wait_ge(w1_in, 80)
            with pe.Fori(0, B) as b:
                def scratch(u):
                    if use[u] >= 2:
                        pe.wait_ge(drained, b * NU + use[u] - 1)
                    return ps[:, bank(u), :]

                def turn(u, src):
                    to = scratch(u)
                    for t in range(NT):
                        mm = nc.tensor.transpose(to[:, t * P:(t + 1) * P], src(t), ident)
                    mm.then_inc(scr_full, 1)

                def hidden(n):
                    for k, (a, m) in enumerate(FCH):
                        i = n * KF + k
                        if i >= 2:
                            pe.wait_ge(h_done, b * NH + i - 1)
                        for which, full in ((0, g_full), (1, u_full)):
                            nc.tensor.matmul(ps[0:m, 2 * which + i % 2, :], gu[:, n, which, a:a + m], hcur[:],
                                             start=True, stop=True).then_inc(full, 1)

                def expert_out(n):
                    pe.wait_ge(h_done, b * NH + n * KF + KF)
                    if n >= 2:
                        pe.wait_ge(acc_done, b * U + n - 1)
                    for t in range(NT):
                        for k, (a, m) in enumerate(FCH):
                            mm = nc.tensor.matmul(ps[:, 6 + n % 2, t * P:(t + 1) * P], hid[0:m, n % 2, k, t * P:(t + 1) * P],
                                                  dn1[0:m, k, n, :], start=(k == 0), stop=(k == KF - 1))
                    mm.then_inc(y_full, 1)

                pe.wait_ge(x_done, b + 1)
                turn("xT", lambda t: xcur[:, t * P:(t + 1) * P])
                pe.wait_ge(z_done, b + 1)
                turn("zT", lambda t: z[:, t, :])
                pe.wait_ge(drained, b * NU + use["zT"] + 1)
                to = scratch("rt")
                for t in range(NT):
                    mm = nc.tensor.matmul(to[:, t * E:(t + 1) * E], hcur[:, t * P:(t + 1) * P], rw[:], start=True, stop=True)
                mm.then_inc(scr_full, 1)
                hidden(0)
                for n in range(1, U):
                    hidden(n)
                    expert_out(n - 1)
                expert_out(U - 1)
                pe.wait_ge(acc_done, b * U + U)
                turn("aT", lambda t: acc[:, t, :])
                pe.wait_ge(drained, b * NU + use["aT"] + 1)
                turn("fT", lambda t: fin[:, t * P:(t + 1) * P])

        @block.scalar
        def _(act):
            with act.Fori(0, B) as b:
                act.wait_ge(m_done, b + 1)
                nc.scalar.activation(pb[:], pb[:], ACT.Exp).then_inc(pe_done, 1)
                for n in range(U):
                    for k, (a, m) in enumerate(FCH):
                        i = n * KF + k
                        act.wait_ge(g_full, b * NH + i + 1)
                        if i >= 2:
                            act.wait_ge(h_done, b * NH + i - 1)
                        nc.scalar.activation(sg[0:m, i % 2, :], ps[0:m, i % 2, :], ACT.Silu).then_inc(s_done, 1)

        @block.vector
        def _(dve):
            with dve.Fori(0, B) as b:
                k_ = [0]

                def then(ins):
                    k_[0] += 1
                    ins.then_inc(dch, 1)
                    dve.wait_ge(dch, b * NDCH + k_[0])

                def full(u):
                    dve.wait_ge(scr_full, b * NU + use[u] + 1)
                    return ps[:, bank(u), :]

                nc.vector.tensor_copy(mc[:], mods[:, 1, :, bass.ds(b, 1)].rearrange("p m o -> p (m o)"))
                nc.vector.tensor_copy(xcur[:], xT[:, bass.ds(b, 1), :].rearrange("p o s -> p (o s)")).then_inc(x_done, 1)
                src = full("xT")
                for t in range(NT):
                    ins = nc.vector.bn_stats(st6[:, t, :], src[:, t * P:(t + 1) * P])
                then(ins)
                dve.sem_inc(g["dve_passed"], 1)
                for t in range(NT):
                    ins = nc.vector.bn_aggr(mv[:, t, :], st6[:, t, :])
                then(ins)
                nc.vector.tensor_scalar(ve[:], mv[:, :, 1], 1e-5, None, ALU.add).then_inc(var_done, 1)
                dve.wait_ge(rstd_done, b + 1)
                for t in range(NT):
                    ins = nc.vector.tensor_scalar(z[:, t, :], src[:, t * P:(t + 1) * P], mv[:, t, 0:1], rs[:, t:t + 1], ALU.subtract, ALU.mult)
                ins.then_inc(z_done, 1)
                dve.wait_ge(z_done, b + 1)
                nc.vector.tensor_copy(ve[:], mv[:, :, 1]).then_inc(drained, 1)
                nc.vector.tensor_scalar(hcur[:], full("zT"), mc[:, CB:CB + 1], mc[:, SB:SB + 1], ALU.mult, ALU.add).then_inc(drained, 1)
                src = full("rt")[:, 0:NT * E].rearrange("p (t e) -> p t e", e=E)
                then(nc.vector.tensor_reduce(rs[:], src, AX, ALU.max))
                nc.vector.tensor_tensor(pb[:], src, rs[:].unsqueeze(2).to_broadcast([P, NT, E]), ALU.subtract).then_inc(m_done, 1)
                dve.wait_ge(m_done, b + 1)
                nc.vector.tensor_copy(ve[:], mv[:, :, 1]).then_inc(drained, 1)
                dve.wait_ge(pe_done, b + 1)
                then(nc.vector.tensor_reduce(rs[:], pb[:], AX, ALU.add))
                then(nc.vector.reciprocal(rs[:], rs[:]))
                then(nc.vector.tensor_tensor(pb[:], pb[:], rs[:].unsqueeze(2).to_broadcast([P, NT, E]), ALU.mult))
                dve.sem_inc(g["dve_passed"], 1)
                for t in range(NT):
                    ins = nc.vector.max(mx8[:, t, :], pb[:, t, :])
                then(ins)
                dve.sem_inc(g["dve_passed"], 1)
                for t in range(NT):
                    ins = nc.vector.max_index(ix8[:, t, :], mx8[:, t, :], pb[:, t, :])
                then(ins)
                then(nc.vector.tensor_tensor(ve[:], mx8[:, :, 0], mx8[:, :, 1], ALU.add))
                then(nc.vector.tensor_scalar(ve[:], ve[:], 1e-20, None, ALU.add))
                nc.vector.tensor_copy(ixf[:], ix8[:])
                then(nc.vector.reciprocal(rs[:], ve[:]))
                then(nc.vector.tensor_tensor(tv[:], mx8[:, :, 0:2], rs[:].unsqueeze(2).to_broadcast([P, NT, 2]), ALU.mult))
                iota = consts[:, IOTA:IOTA + E].unsqueeze(1).to_broadcast([P, NT, E])
                for i in range(2):
                    ins = nc.vector.tensor_tensor(eq[:, i], iota, ixf[:, :, i:i + 1].to_broadcast([P, NT, E]), ALU.is_equal)
                then(ins)
                for i in range(2):
                    ins = nc.vector.tensor_tensor(eq[:, i], eq[:, i], tv[:, :, i:i + 1].to_broadcast([P, NT, E]), ALU.mult)
                then(ins)
                then(nc.vector.tensor_tensor(wt[:], eq[:, 0], eq[:, 1], ALU.add))

                def gated(n):
                    for k, (a, m) in enumerate(FCH):
                        i = n * KF + k
                        if n >= 2 and k == 0:
                            dve.wait_ge(y_full, b * U + n - 1)
                        dve.wait_ge(u_full, b * NH + i + 1)
                        dve.wait_ge(s_done, b * NH + i + 1)
                        nc.vector.tensor_tensor(hid[0:m, n % 2, k, :], ps[0:m, 2 + i % 2, :], sg[0:m, i % 2, :], ALU.mult).then_inc(h_done, 1)

                def accumulate(n):
                    dve.wait_ge(y_full, b * U + n + 1)
                    y = ps[:, 6 + n % 2, :]
                    if n == 0:
                        ins = nc.vector.tensor_copy(acc[:].rearrange("p t d -> p (t d)"), y)
                    else:
                        for t in range(NT):
                            ins = nc.vector.scalar_tensor_tensor(acc[:, t, :], y[:, t * P:(t + 1) * P], wt[:, t, n - 1:n],
                                                                 acc[:, t, :], ALU.mult, ALU.add)
                    ins.then_inc(acc_done, 1)
                    dve.wait_ge(acc_done, b * U + n + 1)

                gated(0)
                for n in range(1, U):
                    gated(n)
                    accumulate(n - 1)
                accumulate(U - 1)
                nc.vector.scalar_tensor_tensor(fin[:], full("aT"), mc[:, GX:GX + 1], xcur[:], ALU.mult, ALU.add).then_inc(drained, 1)
                src = full("fT")
                dve.wait_ge(stored, 16 * (b + 1))
                nc.vector.tensor_copy(outb[:].rearrange("p t d -> p (t d)"), src).then_inc(out_done, 1)
                dve.wait_ge(out_done, b + 1)
                nc.vector.tensor_copy(ve[:], mv[:, :, 1]).then_inc(drained, 1)
                assert k_[0] == NDCH, k_


DVE_CHAIN1 = 15


def _layout(i):
    def cols(a):
        return np.ascontiguousarray(np.asarray(a).reshape(-1, P).T)

    a = {k: np.asarray(v) for k, v in i.items()}
    eye = np.eye(P, dtype=np.float32)
    blocks = np.kron(np.eye(LH), np.ones((LD, LD))).astype(np.float32)
    hsel = np.kron(np.eye(LH), np.ones((LD, 1))).astype(np.float32)
    iota = np.tile(np.arange(E, dtype=np.float32), (P, 1))
    consts = np.concatenate([eye, blocks, hsel, iota, np.ones((P, 32), np.float32)], 1)
    vecs = np.concatenate([cols(a[k]) for k in (
        "L0_attn_b_out", "L0_attn_ln_gamma", "L0_attn_ln_beta", "L0_ffn_gate_bi", "L0_ffn_exp_bi",
        "L1_attn_gf", "L1_attn_bef", "L0_c", "L1_c")], 1)

    def chunks(w):
        w = w.reshape(w.shape[:-2] + (w.shape[-2] // P, P, w.shape[-1]))
        return np.ascontiguousarray(np.moveaxis(w, -2, 0))

    lw = np.concatenate(
        [a["L1_attn_Wq"], a["L1_attn_Wk"], a["L1_attn_Wv"], a["L1_attn_Wo"], a["L1_attn_W1"],
         np.moveaxis(a["L1_attn_W2"].reshape(LAYERS, LFC, P, D), 1, 2).reshape(LAYERS, P, LFC * D)]
        + [np.moveaxis(a[k].reshape(LAYERS, -1, P), 1, 2) for k in (
            "L1_attn_bq", "L1_attn_bo", "L1_attn_g1", "L1_attn_be1", "L1_attn_g2", "L1_attn_be2",
            "L1_attn_c1", "L1_attn_c2")], 2)
    gate = np.concatenate([a["L1_ffn_shared_gate"][None], a["L1_ffn_expert_gate"]])
    up = np.concatenate([a["L1_ffn_shared_up"][None], a["L1_ffn_expert_up"]])
    down = np.concatenate([a["L1_ffn_shared_down"][None], a["L1_ffn_expert_down"]])
    gu = np.stack([np.transpose(gate, (2, 0, 1)), np.transpose(up, (2, 0, 1))], 2)
    return {
        "x": a["L0_attn_x"], "vecs": vecs, "consts": consts,
        "wmod": np.stack([a["L0_wmod"], a["L1_wmod"]], 1),
        "wqkv": a["L0_attn_w_qkv"].reshape(D, 3, HEADS * DH),
        "wout": chunks(a["L0_attn_w_out"]),
        "gwi": a["L0_ffn_gate_wi"], "gwo": chunks(a["L0_ffn_gate_wo"]), "gbo": a["L0_ffn_gate_bo"],
        "ewi": np.transpose(a["L0_ffn_exp_wi"], (1, 0, 2)), "ewo": chunks(a["L0_ffn_exp_wo"]),
        "ebo": a["L0_ffn_exp_bo"],
        "lw": lw, "bkv": np.concatenate([a["L1_attn_bk"], a["L1_attn_bv"]], 1),
        "rw": a["L1_ffn_gate_w"].T, "gu": gu, "dn": np.transpose(down, (2, 0, 1)),
    }


def kernel(**inputs):
    from concourse import bacc
    from concourse.bass_utils import run_bass_kernel_spmd

    nc = bacc.Bacc("TRN2", target_bir_lowering=False, num_devices=1)
    arrays = {f"in_{k}": np.ascontiguousarray(v) for k, v in _layout(inputs).items()}
    ins = {k[3:]: nc.dram_tensor(k, v.shape, mybir.dt.from_np(v.dtype), kind="ExternalInput").ap()
           for k, v in arrays.items()}
    out = nc.dram_tensor("out_x", (B, S, D), F32, kind="ExternalOutput").ap()
    build(nc, ins, out)
    r = run_bass_kernel_spmd(nc, [arrays], core_ids=[0])
    return r.results[0]["out_x"]
```

```python
from contextlib import ExitStack

import numpy as np

import concourse.bass as bass
from concourse import mybir

F32 = mybir.dt.float32
F32R = mybir.dt.float32r
U32 = mybir.dt.uint32
ALU = mybir.AluOpType
ACT = mybir.ActivationFunctionType
AX = mybir.AxisListType.X

P = 128
B, S, D = 4, 512, 128
NT = S // P

HEADS, DH = 32, 32
HC = P // DH
NC = HEADS // HC
SCALE = DH ** -0.5
E = 8
FF0 = 512
FC = FF0 // P
SELU_L = 1.0507009873554805
SELU_A = 1.6732632423543772
LAYERS, LH = 8, 16
LD = D // LH
LFF = 512
LFC = LFF // P
U = 1 + E
FF1 = 352
FCH = [(0, 128), (128, 128), (256, 96)]

BO0, GAM0, BET0, GBI, EBI, GF, BEF, C0, C1 = 0, 1, 2, 3, 7, 39, 40, 41, 45
VECS = 49
IDENT, BLOCKS, HSEL, IOTA, ONES, PICK = 0, 128, 256, 272, 280, 408
CONSTS = 423
WQ, WKV, WO, W1, W2 = 0, 128, 384, 512, 1024
LV = 1536
BQ, LBO, LG1, LBE1, LG2, LBE2, LC1, LC2 = LV, LV + 1, LV + 2, LV + 3, LV + 4, LV + 5, LV + 6, LV + 10
LW = LV + 11
SA, CA, GG, GB, SB, CB, GX = range(7)
NM = 7


def build(nc, ins, out):
    x_in, vecs_in, consts_in, wmod_in, wqkv_in, wout_in = (ins[k] for k in ("x", "vecs", "consts", "wmod", "wqkv", "wout"))
    gwi_in, gwo_in, gbo_in, ewi_in, ewo_in, ebo_in = (ins[k] for k in ("gwi", "gwo", "gbo", "ewi", "ewo", "ebo"))
    lw_in, bkv_in, rw_in, gu_in, dn_in = (ins[k] for k in ("lw", "bkv", "rw", "gu", "dn"))

    x_tok = x_in.rearrange("b (t p) d -> b p t d", p=P)
    out_tok = out.rearrange("b (t p) d -> b p t d", p=P)

    with ExitStack() as ctx:
        def sb(name, shape, dt=F32, at=ctx):
            return at.enter_context(nc.sbuf_tensor(name, shape, dt))

        def sem(name, at=ctx):
            return at.enter_context(nc.semaphore(name))

        ps = ctx.enter_context(nc.psum_tensor("ps", [P, 8, 512], F32))
        consts = sb("consts", [P, CONSTS])
        vecs = sb("vecs", [P, VECS])
        mods = sb("mods", [P, 2, NM, B])
        nhalf = sb("nhalf", [P, NT])
        xT = sb("xT", [P, B, S])
        dve_passed, sp_passed, pool_passed = sem("dve_passed"), sem("sp_passed"), sem("pool_passed")
        ident = consts[:, IDENT:IDENT + P]

        block0(nc, locals())
        rw = sb("rw", [P, E])
        gu = sb("gu", [P, U, 2, FF1])
        h = sb("h", [P, B, S])
        dn1 = sb("dn1", [P, len(FCH), U, D])
        w1_in = sem("experts1_landed")
        layers(nc, locals())
        experts1(nc, locals())


def setup(nc, g):
    ps, consts, vecs, mods, nhalf, wmod = (g[k] for k in ("ps", "consts", "vecs", "mods", "nhalf", "wmod"))
    with ExitStack() as ctx:
        sc = ctx.enter_context(nc.sbuf_tensor("silu_c", [P, 2, B], F32))
        raw = ctx.enter_context(nc.sbuf_tensor("mod_raw", [P, 2, 6, B], F32))
        gate = ctx.enter_context(nc.sbuf_tensor("gate_abs", [P, 2, 2, B], F32))
        sign = ctx.enter_context(nc.sbuf_tensor("gate_sign", [P, 2, 2, B], F32))
        small_in = ctx.enter_context(nc.semaphore("small_in"))
        wmod_in = ctx.enter_context(nc.semaphore("wmod_landed"))
        silu_done = ctx.enter_context(nc.semaphore("silu_done"))
        mod_full = ctx.enter_context(nc.semaphore("mod_full"))
        chain = ctx.enter_context(nc.semaphore("setup_chain"))
        block = ctx.enter_context(nc.Block())

        @block.sync
        def _(sp):
            sp.dma_start(vecs[:], g["vecs_in"]).then_inc(small_in, 16)
            sp.dma_start(wmod, g["wmod_in"]).then_inc(wmod_in, 16)
            sp.dma_start(consts[:], g["consts_in"]).then_inc(small_in, 16)
            sp.dma_start(g["xtok"][:], g["x_tok"][0]).then_inc(g["x_land"], 16)
            sp.dma_start(g["wqkv"][:], g["wqkv_in"]).then_inc(g["w_in"], 16)

        @block.scalar
        def _(act):
            act.wait_ge(small_in, 32)
            nc.scalar.activation(sc[:].rearrange("p l b -> p (l b)"), vecs[:, C0:C0 + 2 * B],
                                 ACT.Silu).then_inc(silu_done, 1)

        @block.tensor
        def _(pe):
            pe.wait_ge(silu_done, 1)
            pe.wait_ge(wmod_in, 16)
            for lv in range(2):
                for k in range(6):
                    at = (lv * 6 + k) * B
                    mm = nc.tensor.matmul(ps[:, 0, at:at + B], wmod[:, lv, k * D:(k + 1) * D],
                                          sc[:, lv, :], start=True, stop=True)
            mm.then_inc(mod_full, 1)

        @block.vector
        def _(dve):
            n = [0]

            def then(ins):
                n[0] += 1
                ins.then_inc(chain, 1)
                dve.wait_ge(chain, n[0])

            nc.vector.memset(nhalf[:], -0.5)
            dve.wait_ge(mod_full, 1)
            then(nc.vector.tensor_copy(raw[:].rearrange("p l k b -> p (l k b)"), ps[:, 0, 0:12 * B]))
            for lv in range(2):
                ga = raw[:, lv, 2:6:3, :]
                then(nc.vector.tensor_scalar(gate[:, lv], ga, -1.0, None, ALU.mult))
                then(nc.vector.tensor_tensor(gate[:, lv], gate[:, lv], ga, ALU.max))
                then(nc.vector.tensor_scalar(gate[:, lv], gate[:, lv], 0.25, None, ALU.max))
                then(nc.vector.tensor_scalar(sign[:, lv], ga, 0.0, 2.0, ALU.is_ge, ALU.mult))
                then(nc.vector.tensor_scalar(sign[:, lv], sign[:, lv], -1.0, None, ALU.add))
                then(nc.vector.tensor_tensor(gate[:, lv], gate[:, lv], sign[:, lv], ALU.mult))
                dve.wait_ge(small_in, 32)
                gamma, beta = ((GAM0, BET0), (GF, BEF))[lv]
                nc.vector.tensor_scalar(mods[:, lv, GG, :], gate[:, lv, 0, :], vecs[:, gamma:gamma + 1], None, ALU.mult)
                nc.vector.tensor_scalar(mods[:, lv, GB, :], gate[:, lv, 0, :], vecs[:, beta:beta + 1], None, ALU.mult)
                nc.vector.tensor_copy(mods[:, lv, GX, :], gate[:, lv, 1, :])
                nc.vector.tensor_copy(mods[:, lv, SA:SB + 1:SB - SA, :], raw[:, lv, 0:4:3, :])
                nc.vector.tensor_scalar(mods[:, lv, CA:CB + 1:CB - CA, :], raw[:, lv, 1:5:3, :], 1.0, None, ALU.add)


def block0(nc, g):
    ps, consts, vecs, mods, nhalf, xT, ident = (g[k] for k in ("ps", "consts", "vecs", "mods", "nhalf", "xT", "ident"))
    dve_passed, sp_passed = g["dve_passed"], g["sp_passed"]
    RING = 3
    PR = 3
    RE = NC // 2
    with ExitStack() as ctx:
        def sb(name, shape, dt=F32):
            return ctx.enter_context(nc.sbuf_tensor(name, shape, dt))

        def sem(name):
            return ctx.enter_context(nc.semaphore(name))

        wqkv = sb("wqkv", [P, 3, HEADS * DH])
        wout = sb("wout", [P, NC, D])
        gwi = sb("gwi", [P, FF0])
        gwo = sb("gwo", [P, FC, D])
        gbo = sb("gbo", [P, D])
        ewi = sb("ewi", [P, E, FF0])
        ewo = sb("ewo", [P, E, FC, D])
        ebo = sb("ebo", [E, D])
        bexp = sb("bexp", [P, (1 + E) * FC])
        mh = sb("mod_head", [P, NM])
        mc = sb("mod_cur", [P, NM])
        xtok = sb("xtok", [P, NT, D])
        tok = sb("tok", [P, NT, D])
        xa = sb("xa", [P, S])
        xcur = sb("xcur", [P, S])
        xg = sb("xg", [P, S])
        ha = sb("ha", [P, S])
        hcur = sb("hcur", [P, S])
        v = sb("v", [P, NT, HEADS * DH])
        hl = sb("hl", [P, 2, 4, S], F32R)
        stk = sb("stk", [P, RING, 2, HC, S], F32R)
        mcol = sb("mcol", [P, 2, HC * NT])
        mrow = sb("mrow", [HC * NT, 2, P], F32R)
        pr = sb("probs", [P, PR, HC, S])
        rden = sb("rden", [P, 2, S])
        oT = sb("oT", [P, NC, S])
        st6 = sb("st6", [P, 2, NT, 6])
        mv = sb("mv", [P, 2, NT, 2])
        ve = sb("ve", [P, 2, NT])
        rs = sb("rs", [P, 2, NT])
        hid = pr[:, 0:2]
        eb, rb = oT[:, 0:NC // 2], oT[:, NC // 2:]
        lgt = xg[:].rearrange("p (t d) -> p t d", d=D)
        mx8 = sb("mx8", [P, NT, 8])
        ix8 = sb("ix8", [P, NT, 8], U32)
        ixf = sb("ixf", [P, NT, 8])
        tv = sb("tv", [P, NT, 2])
        eq = sb("eq", [P, 2, NT, E])
        wt = sb("wt", [P, NT, E])
        wl = sb("wl", [P, NT, E])
        tsum, rsum = sb("top_sum", [P, NT]), sb("top_inv", [P, NT])
        wT = tok[0:E].rearrange("p t d -> p (t d)")
        acc = xg[:].rearrange("p (t d) -> p t d", d=D)

        w_in, w2_in, ones_set = sem("attention_weights_landed"), sem("expert_weights_landed"), sem("ones_set")
        bias_done = sem("bias_done")
        x_land = sem("x_landed")
        var_done, rstd_done, z_done = ([sem(f"{n}_{i}") for i in range(2)] for n in ("var_done", "rstd_done", "z_done"))
        chain_full, chain_drained = sem("chain_full"), sem("chain_drained")
        scr_full, drained = sem("scratch_full"), sem("scratch_drained")
        hi_done, v_full, v_done = sem("hi_done"), sem("values_full"), sem("values_done")
        stk_in = [sem(f"stack_landed_{i}") for i in range(RING)]
        m_in = [sem(f"max_landed_{i}") for i in range(2)]
        st_full, p_done, pv_done = sem("scores_full"), sem("probs_done"), sem("pv_done")
        rden_done, o_done = sem("rden_done"), sem("o_done")
        hid_full, r_done, h_done = sem("hidden_full"), sem("relu_done"), sem("hidden_done")
        y_full, acc_done, wt_done = sem("expert_out_full"), sem("acc_done"), sem("gates_done")
        dch, ln_done, den_done, sums_full = sem("dve_chain"), sem("ln_done"), sem("den_done"), sem("weight_sums_full")
        stats_done, aggr_done = ([sem(f"{n}_{i}") for i in range(2)] for n in ("stats_done", "aggr_done"))

        setup(nc, {**g, "wmod": pr[:, 0, 0:3, :].rearrange("p l n -> p (l n)").rearrange("p (l n) -> p l n", l=2),
                   "xtok": xtok, "wqkv": wqkv, "x_land": x_land, "w_in": w_in})

        vs = [("v", t, h) for t in range(NT) for h in range(2)]
        ms = [("mx", 0, i) for i in range(16)]
        HEAD = [("hx",), ("hn",), ("hz",)] + [(n, c) for c in range(RING) for n in "qk"] + vs + ms + [("mT", 0)]
        slots = {}
        for c in range(NC):
            for kt in range(NT):
                u = []
                if kt == 3 and c + RING < NC:
                    u += [("q", c + RING), ("k", c + RING)]
                if c + 1 < NC:
                    u += [("mx", c + 1, i) for i in (range(0, 6), range(6, 11), range(11, 16), [])[kt]]
                    if kt == 3:
                        u += [("mT", c + 1)]
                u += {(5, 3): [("hx",)], (6, 3): [("hn",)], (7, 0): [("hz",)], (7, 1): [("q", 0), ("k", 0)], (7, 3): [("q", 1), ("k", 1)]}.get((c, kt), [])
                slots[c, kt] = u

        def hid_(n, *fs):
            return [("hid", n, f) for f in fs]

        tail = [("o",), vs[0], ("sT",), vs[1], ms[0], vs[2], ("sZ",), ms[1], ("zB",), vs[3], ("x2T",), vs[4], ms[2], vs[5], ("x2Z",),
                ms[3], ("zC",), vs[6], *hid_(0, 0, 1, 2, 3), vs[7], ms[4], *hid_(1, 0, 1), ("lg",), *hid_(1, 2, 3), ("top",),
                *hid_(2, 0, 1, 2, 3), ("eo", 1), *ms[5:7], ("wT",), ms[7], ("bw",), ("acc", 1)]
        for n in range(3, 1 + E):
            m1, m2 = (ms[2 * n + 2:2 * n + 3], ms[2 * n + 3:2 * n + 4]) if n < 7 else ([("mT", 0)] if n == 7 else [], [])
            tail += [*hid_(n, 0, 1), *m1, *hid_(n, 2, 3), *m2, ("eo", n - 1), ("acc", n - 1)]
            tail += {7: [("q", 2)], 8: [("k", 2)]}.get(n, [])
        tail += [("eo", E), ("acc", E), ("aT",)]
        plan = [("start",)]
        for n in range(NC * NT):
            c, kt = n // NT, n % NT
            first = [u for u in slots[c, kt] if u[0] != "mx" and u != ("mT", c + 1)]
            mx = [u for u in slots[c, kt] if u[0] == "mx"]
            turn = [u for u in slots[c, kt] if u == ("mT", c + 1)]
            plan += [("s", n, 0)] + mx[0:1] + [("s", n, 1)] + turn + mx[1:2]
            plan += ([("den", n - 1)] + first[0:1] + mx[2:4] + [("pv", n - 1)] + first[1:2] + mx[4:]) if n else mx[2:]
            if kt == 0 and c:
                plan += [("att", c - 1)]
        plan += [("den", NC * NT - 1), ("pv", NC * NT - 1), ("att", NC - 1)] + tail
        BODY = [("lg",), ("wT",), ("bw",), ("aT",)]
        order = [u for u in plan if u[0] in ("q", "k", "mx", "mT", "hx", "hz") or u in BODY]
        use = {u: i for i, u in enumerate(order)}
        NU = len(order)
        CH = {u: i for i, u in enumerate([("o",), ("sT",), ("zB",), ("x2T",), ("zC",)])}
        NST = NC * NT
        NSL = [len(range(i, NC, RING)) for i in range(RING)]
        LAND = 3 * HC * 16
        NH = (1 + E) * FC

        def bank(u):
            return ps[:, 4 + use[u] % 2, :]

        def cbank(u):
            return ps[:, CH[u] % 4, :]

        def walk(own, nxt, do, skip=None):
            out = 0
            for u in plan:
                if (nxt if u in HEAD else own) is None:
                    out += u in use
                    continue
                if out and u in use:
                    if skip:
                        skip(use[u] - out, out)
                    out = 0
                do(u)
            if out and skip:
                skip(NU - out, out)

        def phases(eng, phase):
            phase(None, 0, 0)
            with eng.Fori(0, B - 1) as b:
                phase(b, b + 1, b * NU + NU)
            phase(B - 1, None, B * NU)

        block = ctx.enter_context(nc.Block())

        @block.sync
        def _(sp):
            for dst, src in ((gwi, "gwi_in"), (gwo, "gwo_in"), (gbo, "gbo_in"), (ewi, "ewi_in"), (ewo, "ewo_in"), (ebo, "ebo_in")):
                sp.dma_start(dst[:], g[src].partition_broadcast(P) if dst is gbo else g[src]).then_inc(w2_in, 16)
            sp.dma_start(wout[:], g["wout_in"]).then_inc(w2_in, 16)

            def phase(own, nxt, base):
                def do(u):
                    if u[0] == "k":
                        c = u[1]
                        sp.wait_ge(drained, base + use[u] + 1)
                        sp.sem_inc(sp_passed, 1)
                        if own is not None:
                            last = c - RING if c >= RING else max(i for i in range(NC) if i % RING == c)
                            sp.wait_ge(st_full, own * 2 * NST + 2 * NT * (last + 1))
                            sp.sem_inc(sp_passed, 1)
                        for j in range(HC):
                            for r, (qs, ks) in enumerate(((0, 2), (1, 2), (0, 3))):
                                sp.dma_start(stk[DH * r:DH * r + DH, c % RING, :, j, :].bitcast(F32),
                                             hl[DH * j:DH * j + DH, c % 2, qs:ks + 1:ks - qs, :].bitcast(F32)).then_inc(stk_in[c % RING], 16)
                    elif u[0] == "mT":
                        c = u[1]
                        sp.wait_ge(drained, base + use[u] + 1)
                        sp.sem_inc(sp_passed, 1)
                        sp.dma_start(stk[96:97, c % RING, 0, :, :].rearrange("p j (t n) -> p (j t) n", n=P).bitcast(F32),
                                     mrow[:, c % 2, :].bitcast(F32)).then_inc(m_in[c % 2], 16)
                    elif u[0] == "start" and nxt is not None:
                        sp.dma_start(xtok[:], g["x_tok"][nxt]).then_inc(x_land, 16)

                walk(own, nxt, do)

            phases(sp, phase)

        @block.gpsimd
        def _(pool):
            def phase(own, nxt, base):
                def do(u):
                    if u[0] == "hx":
                        pool.wait_ge(var_done[0], nxt + 1)
                        nc.gpsimd.tensor_tensor(rs[:, 0], ve[:, 0], nhalf[:], ALU.pow).then_inc(rstd_done[0], 1)
                    elif u[0] in ("sT", "x2T"):
                        pool.wait_ge(var_done[1], 2 * own + (1 if u[0] == "sT" else 2))
                        nc.gpsimd.tensor_tensor(rs[:, 1], ve[:, 1], nhalf[:], ALU.pow).then_inc(rstd_done[1], 1)

                walk(own, nxt, do)

            phases(pool, phase)

        @block.tensor
        def _(pe):
            pe.wait_ge(w_in, 16)

            def phase(own, nxt, base):
                def scratch(u):
                    if own is not None or use[u] >= 2:
                        pe.wait_ge(drained, base + (use[u] - 1))
                    return bank(u)

                def turn(to, src, done):
                    for t in range(NT):
                        mm = nc.tensor.transpose(to[:, t * P:(t + 1) * P], src(t), ident)
                    mm.then_inc(done, 1)

                def chain(u, src):
                    pe.wait_ge(chain_drained, own * len(CH) + CH[u])
                    turn(cbank(u), src, chain_full)

                def scores(n, half):
                    c, kt = n // NT, n % NT
                    if n:
                        pe.wait_ge(p_done, own * 2 * NST + (2 * n + half - 1))
                    if kt == 0 and half == 0:
                        pe.wait_ge(m_in[c % 2], 16 * (own * (NC // 2) + (c // 2 + 1)))
                    for jj in range(2):
                        j = 2 * half + jj
                        mm = nc.tensor.matmul(ps[:, 2 * half + jj, :], stk[0:97, c % RING, 1, j, kt * P:(kt + 1) * P],
                                              stk[0:97, c % RING, 0, j, :], start=True, stop=True)
                    mm.then_inc(st_full, 1)

                def values(n, what):
                    c, kt = n // NT, n % NT
                    if what == "den":
                        pe.wait_ge(p_done, own * 2 * NST + (2 * n + 2))
                    if kt == 0 and c:
                        pe.wait_ge(o_done if what == "pv" else ln_done, own * NC + c)
                    for j in range(HC):
                        h = HC * c + j
                        w, to = (v[:, kt, h * DH:(h + 1) * DH], 6) if what == "pv" else (consts[:, ONES:ONES + DH], 7)
                        mm = nc.tensor.matmul(ps[DH * j:DH * j + DH, to, :], w, pr[:, n % PR, j, :],
                                              start=(kt == 0), stop=(kt == NT - 1), tile_position=(0, DH * j))
                    mm.then_inc(pv_done if what == "pv" else den_done, 1)

                def do(u):
                    k = u[0]
                    if k == "hx":
                        pe.wait_ge(x_land, 16 * (nxt + 1))
                        turn(scratch(u), lambda t: xtok[:, t, :], scr_full)
                    elif k == "hz":
                        pe.wait_ge(z_done[0], nxt + 1)
                        turn(scratch(u), lambda t: xtok[:, t, :], scr_full)
                    elif k == "v":
                        t, h = u[1:]
                        i = vs.index(u)
                        if i >= 2:
                            pe.wait_ge(v_done, nxt * len(vs) + (i - 1))
                        nc.tensor.matmul(ps[:, 6 + i % 2, :], ha[:, t * P:(t + 1) * P], wqkv[:, 2, h * 512:(h + 1) * 512],
                                         start=True, stop=True).then_inc(v_full, 1)
                    elif k in ("q", "k"):
                        c = u[1]
                        to = scratch(u)
                        if u == ("q", 0):
                            pe.wait_ge(drained, base + (use["hz",] + 1))
                        nc.tensor.matmul(to, wqkv[:, "qk".index(k), c * P:(c + 1) * P], ha[:], start=True, stop=True).then_inc(scr_full, 1)
                    elif k == "mx":
                        c, i = u[1:]
                        j, qt = i // NT, i % NT
                        to = scratch(u)
                        if i == 0:
                            who = own if c else nxt
                            pe.wait_ge(stk_in[c % RING], who * LAND * NSL[c % RING] + LAND * (c // RING + 1))
                        nc.tensor.matmul(to, stk[0:96, c % RING, 0, j, qt * P:(qt + 1) * P], stk[0:96, c % RING, 1, j, :],
                                         start=True, stop=True).then_inc(scr_full, 1)
                    elif k == "mT":
                        c = u[1]
                        to = scratch(u)
                        pe.wait_ge(drained, base + (use["mx", c, 15] + 1))
                        nc.tensor.transpose(to[0:HC * NT, 0:P], mcol[:, c % 2, :], ident).then_inc(scr_full, 1)
                    elif k == "s":
                        scores(*u[1:])
                    elif k in ("pv", "den"):
                        values(u[1], k)
                    elif k == "o":
                        pe.wait_ge(o_done, own * NC + NC)
                        for c in range(NC):
                            mm = nc.tensor.matmul(cbank(u), wout[:, c, :], oT[:, c, :], start=(c == 0), stop=(c == NC - 1))
                        mm.then_inc(chain_full, 1)
                    elif k == "sT":
                        chain(u, lambda t: xg[:, t * P:(t + 1) * P])
                    elif k in ("zB", "zC"):
                        pe.wait_ge(z_done[1], 2 * own + (1 if k == "zB" else 2))
                        chain(u, lambda t: tok[:, t, :])
                    elif k == "x2T":
                        chain(u, lambda t: xcur[:, t * P:(t + 1) * P])
                    elif k == "hid":
                        n, f = u[1:]
                        i = n * FC + f
                        if i == 0:
                            pe.wait_ge(chain_drained, own * len(CH) + len(CH))
                        if i >= 4:
                            pe.wait_ge(r_done, own * NH + (i - 3))
                        w = gwi[:, f * P:(f + 1) * P] if n == 0 else ewi[:, n - 1, f * P:(f + 1) * P]
                        nc.tensor.matmul(ps[:, i % 4, :], w, hcur[:], start=True, stop=True).then_inc(hid_full, 1)
                    elif k == "lg":
                        pe.wait_ge(h_done, own * NH + FC)
                        to = scratch(u)
                        for t in range(NT):
                            for f in range(FC):
                                mm = nc.tensor.matmul(to[:, t * P:(t + 1) * P], hid[:, 0, f, t * P:(t + 1) * P], gwo[:, f, :],
                                                      start=(f == 0), stop=(f == FC - 1))
                        mm.then_inc(scr_full, 1)
                    elif k == "wT":
                        pe.wait_ge(wt_done, own + 1)
                        to = scratch(u)
                        for t in range(NT):
                            mm = nc.tensor.transpose(to[0:E, t * P:(t + 1) * P], wt[:, t, :], ident)
                        mm.then_inc(scr_full, 1)
                    elif k == "bw":
                        to = scratch(u)
                        pe.wait_ge(drained, base + (use["wT",] + 1))
                        for t in range(NT):
                            mm = nc.tensor.matmul(to[:, t * P:(t + 1) * P], wT[:, t * P:(t + 1) * P], ebo[:], start=True, stop=True)
                        mm.then_inc(scr_full, 1)
                    elif k == "eo":
                        n = u[1]
                        pe.wait_ge(h_done, own * NH + (n * FC + FC))
                        if n == 1 and nxt is not None:
                            pe.wait_ge(v_done, nxt * len(vs) + len(vs))
                        if n >= 3:
                            pe.wait_ge(acc_done, own * E + (n - 2))
                        for t in range(NT):
                            for f in range(FC):
                                mm = nc.tensor.matmul(ps[:, 6 + n % 2, t * P:(t + 1) * P], hid[:, n % 2, f, t * P:(t + 1) * P],
                                                      ewo[:, n - 1, f, :], start=(f == 0), stop=(f == FC - 1))
                        mm.then_inc(y_full, 1)
                    elif k == "aT":
                        pe.wait_ge(acc_done, own * E + E)
                        turn(scratch(u), lambda t: acc[:, t, :], scr_full)

                def skip(i, n):
                    if own is not None or i:
                        pe.wait_ge(scr_full, base + i)
                    pe.sem_inc(scr_full, n)

                walk(own, nxt, do, skip)
                if own is None:
                    pe.wait_ge(w2_in, 16 * 7)
                    for f in range(FC):
                        nc.tensor.matmul(ps[:, 0, 0:D], consts[:, ONES:ONES + P], gwo[:, f, :], start=(f == 0), stop=(f == FC - 1))
                    for e in range(E):
                        for f in range(FC):
                            mm = nc.tensor.matmul(ps[0:E, 1, 0:D], consts[:, PICK + E - 1 - e:PICK + 2 * E - 1 - e], ewo[:, e, f, :],
                                                  start=(e + f == 0), stop=(e == E - 1 and f == FC - 1))
                    mm.then_inc(sums_full, 1)
                    pe.wait_ge(bias_done, 3)
                    pe.wait_ge(ones_set, 1)

            phases(pe, phase)

        @block.scalar
        def _(act):
            nc.scalar.preload_act_table_set("natural_log_exp_and_others")

            def phase(own, nxt, base):
                def do(u):
                    k = u[0]
                    if k in ("q", "k"):
                        c = u[1]
                        act.wait_ge(scr_full, base + (use[u] + 1))
                        if c >= 2:
                            who = nxt if c < RING else own
                            act.wait_ge(stk_in[(c - 2) % RING], who * (LAND * NSL[(c - 2) % RING]) + LAND * ((c - 2) // RING + 1))
                        nc.scalar.activation(hl[:, c % 2, 2 * (k == "k"), :], bank(u), ACT.Identity).then_inc(hi_done, 1)
                    elif k == "v":
                        t, h = u[1:]
                        i = vs.index(u)
                        act.wait_ge(v_full, nxt * len(vs) + (i + 1))
                        nc.scalar.activation(v[:, t, h * 512:(h + 1) * 512], ps[:, 6 + i % 2, :], ACT.Identity).then_inc(v_done, 1)
                    elif k == "s":
                        n, half = u[1:]
                        if n >= PR and half == 0:
                            act.wait_ge(pv_done, own * NST + (n - PR + 1))
                        act.wait_ge(st_full, own * 2 * NST + (2 * n + half + 1))
                        nc.scalar.activation(pr[:, n % PR, 2 * half:2 * half + 2, :], ps[:, 2 * half:2 * half + 2, :],
                                             ACT.Exp, scale=SCALE).then_inc(p_done, 1)
                    elif k == "att":
                        c = u[1]
                        act.wait_ge(den_done, own * NST + (NT * c + NT))
                        if c >= 2:
                            act.wait_ge(o_done, own * NC + (c - 1))
                        nc.scalar.activation(rden[:, c % 2, :], ps[:, 7, :], ACT.Ln).then_inc(ln_done, 1)
                        act.wait_ge(ln_done, own * NC + (c + 1))
                        nc.scalar.activation(rden[:, c % 2, :], rden[:, c % 2, :], ACT.Exp, scale=-1.0).then_inc(rden_done, 1)
                    elif k == "hid":
                        n, f = u[1:]
                        i = n * FC + f
                        if i == 0:
                            act.wait_ge(bias_done, 1)
                        act.wait_ge(hid_full, own * NH + (i + 1))
                        if i >= RE:
                            act.wait_ge(h_done, own * NH + (i - RE + 1))
                        nc.scalar.activation(eb[:, i % RE, :], ps[:, i % 4, :], ACT.Exp, bias=bexp[:, i:i + 1])
                        nc.scalar.activation(rb[:, i % RE, :], ps[:, i % 4, :], ACT.Relu, bias=vecs[:, GBI + i:GBI + i + 1]).then_inc(r_done, 1)

                walk(own, nxt, do)

            phases(act, phase)

        @block.vector
        def _(dve):
            nc.vector.tensor_scalar(bexp[:], vecs[:, GBI:GBI + NH], float(np.log(SELU_A)), None, ALU.add).then_inc(bias_done, 1)

            def phase(own, nxt, base):
                n_chain = [0]

                def then(ins):
                    n_chain[0] += 1
                    ins.then_inc(dch, 1)
                    dve.wait_ge(dch, own * DVE_CHAIN + n_chain[0])

                def full(u):
                    dve.wait_ge(scr_full, base + (use[u] + 1))
                    return bank(u)

                def cfull(u):
                    dve.wait_ge(chain_full, own * len(CH) + (CH[u] + 1))
                    return cbank(u)

                def statistics(i, src, eps, nth):
                    for t in range(NT):
                        ins = nc.vector.bn_stats(st6[:, i, t, :], src(t))
                    ins.then_inc(stats_done[i], 1)
                    dve.wait_ge(stats_done[i], nth)
                    dve.sem_inc(dve_passed, 1)
                    for t in range(NT):
                        ins = nc.vector.bn_aggr(mv[:, i, t, :], st6[:, i, t, :])
                    ins.then_inc(aggr_done[i], 1)
                    dve.wait_ge(aggr_done[i], nth)
                    nc.vector.tensor_scalar(ve[:, i], mv[:, i, :, 1], eps, None, ALU.add).then_inc(var_done[i], 1)

                def normalise(i, src, to, nth):
                    dve.wait_ge(rstd_done[i], nth)
                    for t in range(NT):
                        ins = nc.vector.tensor_scalar(to[:, t, :], src(t), mv[:, i, t, 0:1], rs[:, i, t:t + 1], ALU.subtract, ALU.mult)
                    ins.then_inc(z_done[i], 1)

                def selu(n, f):
                    i = n * FC + f
                    if n > 2 and f == 0:
                        dve.wait_ge(y_full, own * E + (n - 2))
                    dve.wait_ge(r_done, own * NH + (i + 1))
                    nc.vector.scalar_tensor_tensor(hid[:, n % 2, f, :], eb[:, i % RE, :], SELU_A, rb[:, i % RE, :],
                                                   ALU.min, ALU.add).then_inc(h_done, 1)

                def top():
                    dve.wait_ge(drained, base + (use["lg",] + 1))
                    dve.sem_inc(dve_passed, 1)
                    for t in range(NT):
                        ins = nc.vector.max(mx8[:, t, :], lgt[:, t, :])
                    then(ins)
                    dve.sem_inc(dve_passed, 1)
                    for t in range(NT):
                        ins = nc.vector.max_index(ix8[:, t, :], mx8[:, t, :], lgt[:, t, :])
                    nc.vector.tensor_tensor(tsum[:], mx8[:, :, 0], mx8[:, :, 1], ALU.add)
                    then(ins)
                    then(nc.vector.tensor_copy(ixf[:], ix8[:]))
                    then(nc.vector.reciprocal(rsum[:], tsum[:]))
                    then(nc.vector.tensor_tensor(tv[:], mx8[:, :, 0:2], rsum[:].unsqueeze(2).to_broadcast([P, NT, 2]), ALU.mult))
                    iota = consts[:, IOTA:IOTA + E].unsqueeze(1).to_broadcast([P, NT, E])
                    for i in range(2):
                        ins = nc.vector.tensor_tensor(eq[:, i], iota, ixf[:, :, i:i + 1].to_broadcast([P, NT, E]), ALU.is_equal)
                    then(ins)
                    for i in range(2):
                        ins = nc.vector.tensor_tensor(eq[:, i], eq[:, i], tv[:, :, i:i + 1].to_broadcast([P, NT, E]), ALU.mult)
                    then(ins)
                    then(nc.vector.tensor_tensor(wt[:], eq[:, 0], eq[:, 1], ALU.add))
                    nc.vector.tensor_scalar(wl[:], wt[:], SELU_L, None, ALU.mult).then_inc(wt_done, 1)

                def do(u):
                    k = u[0]
                    if k == "start":
                        dve.wait_ge(drained, base)
                        then(nc.vector.tensor_copy(mc[:], mh[:]))
                        nc.vector.tensor_scalar(xcur[:], xa[:], mc[:, GB:GB + 1], None, ALU.add)
                    elif k == "hx":
                        nc.vector.tensor_copy(mh[:], mods[:, 0, :, bass.ds(nxt, 1)].rearrange("p m o -> p (m o)"))
                        nc.vector.tensor_copy(xa[:], full(u)).then_inc(drained, 1)
                        statistics(0, lambda t: xtok[:, t, :], 1e-5, nxt + 1)
                    elif k == "hn":
                        normalise(0, lambda t: xtok[:, t, :], xtok, nxt + 1)
                    elif k == "hz":
                        nc.vector.tensor_scalar(ha[:], full(u), mh[:, CA:CA + 1], mh[:, SA:SA + 1], ALU.mult, ALU.add).then_inc(drained, 1)
                    elif k in ("q", "k"):
                        c, i = u[1], "qk".index(k)
                        who = nxt if c < RING else own
                        src = full(u)
                        dve.wait_ge(hi_done, who * (2 * NC) + (2 * c + i + 1))
                        nc.vector.tensor_tensor(hl[:, c % 2, 2 * i + 1, :], src, hl[:, c % 2, 2 * i, :].bitcast(F32),
                                                ALU.subtract).then_inc(drained, 1)
                    elif k == "mx":
                        c, i = u[1:]
                        if own is None and i == 0:
                            nc.vector.memset(stk[96:97, :, 1, :, :].bitcast(F32), 1.0).then_inc(ones_set, 1)
                        nc.vector.tensor_reduce(mcol[:, c % 2, i:i + 1], full(u), AX, ALU.max).then_inc(drained, 1)
                    elif k == "mT":
                        c = u[1]
                        src = full(u)
                        nc.vector.tensor_scalar(mrow[:, c % 2, :], src[0:HC * NT, 0:P], -1.0, None, ALU.mult).then_inc(drained, 1)
                    elif k == "att":
                        c = u[1]
                        dve.wait_ge(rden_done, own * NC + (c + 1))
                        dve.wait_ge(pv_done, own * NST + (NT * c + NT))
                        nc.vector.tensor_tensor(oT[:, c, :], ps[:, 6, :], rden[:, c % 2, :], ALU.mult).then_inc(o_done, 1)
                    elif k == "o":
                        nc.vector.tensor_scalar(xg[:], cfull(u), vecs[:, BO0:BO0 + 1], None, ALU.add).then_inc(chain_drained, 1)
                    elif k in ("sT", "x2T"):
                        src = cfull(u)
                        statistics(1, lambda t: src[:, t * P:(t + 1) * P], 1e-6 if k == "sT" else 1e-5, 2 * own + (1 if k == "sT" else 2))
                    elif k in ("sZ", "x2Z"):
                        nth, src = 2 * own + (1 if k == "sZ" else 2), cbank((k[:-1] + "T",))
                        normalise(1, lambda t: src[:, t * P:(t + 1) * P], tok, nth)
                        dve.wait_ge(z_done[1], nth)
                        dve.sem_inc(chain_drained, 1)
                    elif k == "zB":
                        nc.vector.scalar_tensor_tensor(xcur[:], cfull(u), mc[:, GG:GG + 1], xcur[:], ALU.mult, ALU.add).then_inc(chain_drained, 1)
                    elif k == "zC":
                        nc.vector.tensor_scalar(hcur[:], cfull(u), mc[:, CB:CB + 1], mc[:, SB:SB + 1], ALU.mult, ALU.add).then_inc(chain_drained, 1)
                    elif k == "hid":
                        selu(*u[1:])
                    elif k == "lg":
                        nc.vector.scalar_tensor_tensor(lgt[:], full(u).rearrange("p (t d) -> p t d", d=D), SELU_L,
                                                       gbo[:].unsqueeze(1).to_broadcast([P, NT, D]), ALU.mult, ALU.add).then_inc(drained, 1)
                    elif k == "top":
                        top()
                    elif k == "wT":
                        nc.vector.tensor_copy(wT, full(u)[0:E, :]).then_inc(drained, 1)
                    elif k == "bw":
                        nc.vector.tensor_copy(xg[:], full(u)).then_inc(drained, 1)
                        dve.wait_ge(drained, base + (use[u] + 1))
                    elif k == "acc":
                        n = u[1]
                        dve.wait_ge(y_full, own * E + n)
                        for t in range(NT):
                            ins = nc.vector.scalar_tensor_tensor(acc[:, t, :], ps[:, 6 + n % 2, t * P:(t + 1) * P],
                                                                 wl[:, t, n - 1:n], acc[:, t, :], ALU.mult, ALU.add)
                        ins.then_inc(acc_done, 1)
                        dve.wait_ge(acc_done, own * E + n)
                    elif k == "aT":
                        nc.vector.scalar_tensor_tensor(xT[:, bass.ds(own, 1), :].rearrange("p o s -> p (o s)"), full(u), mc[:, GX:GX + 1],
                                                       xcur[:], ALU.mult, ALU.add).then_inc(drained, 1)

                def skip(i, n):
                    if own is not None or i:
                        dve.wait_ge(drained, base + i)
                    dve.sem_inc(drained, n)

                walk(own, nxt, do, skip)
                assert own is None or n_chain[0] == DVE_CHAIN, n_chain
                if own is None:
                    dve.wait_ge(sums_full, 1)
                    nc.vector.scalar_tensor_tensor(gbo[:], ps[:, 0, 0:D], -SELU_L * SELU_A, gbo[:], ALU.mult, ALU.add).then_inc(bias_done, 1)
                    nc.vector.scalar_tensor_tensor(ebo[:], ps[0:E, 1, 0:D], -SELU_L * SELU_A, ebo[:], ALU.mult, ALU.add).then_inc(bias_done, 1)
                    dve.wait_ge(bias_done, 3)

            phases(dve, phase)


DVE_CHAIN = 9


PERIOD = 61.0
EDGES = ("sTin", "zTin", "sTout", "zTout", "sTexp", "zTexp")
STEPS = {
    "tensor": [
        ("sTin", -7.000), ("zTin", -1.600), ("q", 0.524), ("kva", 4.500), ("kvb", 8.037), ("kvs",
        13.979), ("att", 17.281), ("atT", 22.359), ("o", 24.961), ("sT1", 25.854), ("zT1", 31.513),
        ("f0", 34.429), ("f1", 37.485), ("f2", 39.641), ("y0", 40.667), ("y1", 41.119), ("f3", 41.196),
        ("y2", 41.753), ("y3", 44.934), ("sT2", 49.176), ("zT2", 59.615), ("sTout", 61.500), ("zTout",
        66.900), ("sTexp", 68.300), ("zTexp", 73.700)],
    "scalar": [
        ("sTin", -3.400), ("q", 4.798), ("kv", 10.179), ("atT", 23.972), ("sT1", 31.503), ("f0",
        35.839), ("f1", 38.499), ("f2", 40.657), ("f3", 42.707), ("sT2", 56.067), ("sTout", 65.100),
        ("sTexp", 71.900)],
    "vector": [
        ("sTin", -6.500), ("zTin", -1.100), ("phiq", 6.802), ("kva", 7.693), ("kvb", 10.013), ("phik",
        13.694), ("kvs", 13.989), ("att", 19.602), ("o", 25.634), ("sT1", 26.137), ("zT1", 34.419),
        ("y3", 45.120), ("sT2", 55.301), ("zT2", 59.625), ("sTout", 62.000), ("zTout", 67.400),
        ("sTexp", 68.800), ("zTexp", 74.200)],
    "gpsimd": [
        ("sTin", -5.000), ("q", 5.209), ("kv", 10.458), ("sT1", 27.345), ("sT2", 56.057), ("sTout",
        63.500), ("sTexp", 70.300)],
}


def layers(nc, g):
    ps, consts, vecs, mods, nhalf, xT, ident = (g[k] for k in ("ps", "consts", "vecs", "mods", "nhalf", "xT", "ident"))
    h = g["h"]
    LNS = ("in", "1", "2", "out", "exp")
    with ExitStack() as ctx:
        def sb(name, shape, dt=F32):
            return ctx.enter_context(nc.sbuf_tensor(name, shape, dt))

        def sem(name):
            return ctx.enter_context(nc.semaphore(name))

        w = sb("layer_w", [P, 2, LW])
        bkv = sb("layer_bkv", [P, 2, 2 * D])
        bq1 = sb("bq1", [P, 2])
        s = sb("s", [P, B, S])
        z = sb("z", [P, B, NT, D])
        ex = sb("ex", [P, B, S])
        q = sb("q", [P, B, S])
        kv = sb("kv", [P, B, NT, 2 * D + 1])
        kf = sb("kf", [P, B, NT, D])
        kvm = sb("kvm", [P, B, D + LH])
        dn = sb("dn", [P, B, NT, LH])
        hid = sb("layer_hid", [P, B, LFC, S])
        st6 = sb("l_st6", [P, B, NT, 6])
        mv = sb("l_mv", [P, B, NT, 2])
        ve = sb("l_ve", [P, B, 2, NT])
        rs = sb("l_rs", [P, B, NT])
        nm = sb("l_nm", [P, B, NT])
        xg = sb("l_xg", [P, B, S])

        w_in = [sem(f"layer_w_landed_{i}") for i in range(2)]
        names = ("q_full q_exp q_clip q_done kva_full kvb_full kv_done k_exp k_clip k_done kvs_full kvm_done "
                 "att_full den_done rec_done at_done atT_full atT_done o_full o_sum f0_full f1_full f2_full f3_full "
                 "f0_done f1_done f2_done f3_done y_full y_sum bq1_done one_set").split()
        S_ = {k: sem(k) for k in names}
        ln = {k: {x: sem(f"ln_{k}_{x}") for x in ("full", "stats", "aggr", "var", "rs", "rstd", "z", "zfull", "done")
                  if (k, x) != ("in", "done")} for k in LNS}
        ln["in"]["done"] = ln["2"]["done"]
        xg_done = sem("xg_done")
        w_free = sem("layer_w_free")

        def run(eng, steps, part):
            def go(now, l, before):
                for _, _, st, e, earlier in sorted(now):
                    k, par = (0, 0) if st in EDGES else before if earlier else l
                    part(st, e, k, par)

            quarter = PERIOD / B
            placed = [(t + e * quarter, i, st, e) for e in range(B) for i, (st, t) in enumerate(steps)]
            cur = [(t, i, st, e, False) for t, i, st, e in placed if 0 <= t < PERIOD and st not in EDGES]
            prev = [(t - PERIOD, i, st, e, True) for t, i, st, e in placed if t >= PERIOD and st not in EDGES]
            before = [(t, i, st, e, False) for t, i, st, e in placed if st in EDGES[:2]]
            behind = [(t - PERIOD, i, st, e, True) for t, i, st, e in placed if st in EDGES[2:]]
            go(before + cur, (0, 0), None)
            with eng.Fori(0, LAYERS // 2 - 1) as i:
                for k in (1, 2):
                    go(cur + prev, (i * 2 + k, k % 2), (i * 2 + (k - 1), 1 - k % 2))
            go(cur + prev, (LAYERS - 1, 1), (LAYERS - 2, 0))
            go(prev + behind, None, (LAYERS - 1, 1))

        def at(l, e, n=1, k=0):
            return (l * B + e) * n + k + 1

        def which(st):
            return {"sTin": "in", "sT1": "1", "sT2": "2", "sTout": "out", "sTexp": "exp"}[st]

        block = ctx.enter_context(nc.Block())

        @block.sync
        def _(sp):
            def load(l, par):
                sp.dma_start(w[:, par, :], g["lw_in"][l]).then_inc(w_in[par], 16)
                sp.dma_start(bkv[:, par, :], g["bkv_in"][l].partition_broadcast(P)).then_inc(w_in[par], 16)

            load(0, 0)
            load(1, 1)
            sp.dma_start(g["rw"][:], g["rw_in"]).then_inc(g["w1_in"], 16)
            sp.dma_start(g["gu"][:], g["gu_in"]).then_inc(g["w1_in"], 16)
            for k, (a, n) in enumerate(FCH):
                sp.dma_start(g["dn1"][0:n, k, :, :], g["dn_in"][a:a + n]).then_inc(g["w1_in"], 16)
            with sp.Fori(0, LAYERS // 2 - 1) as i:
                for par in range(2):
                    sp.wait_ge(w_free, i * 2 + par + 1)
                    sp.sem_inc(g["sp_passed"], 1)
                    load(i * 2 + par + 2, par)

        @block.tensor
        def _(pe):
            pe.wait_ge(S_["one_set"], 1)

            def part(st, e, l, par):
                A, Bk = ps[:, 2 * e, :], ps[:, 2 * e + 1, :]
                W = w[:, par, :]
                if st == "q":
                    if e == 0:
                        pe.wait_ge(w_in[par], (l - par) * 16 + 32)
                    pe.wait_ge(ln["2"]["done"], at(l, e))
                    nc.tensor.matmul(A, W[:, WQ:WQ + D], h[:, e, :], start=True, stop=True).then_inc(S_["q_full"], 1)
                elif st in ("kva", "kvb"):
                    i, bk = (0, Bk) if st == "kva" else (1, A)
                    if i == 1:
                        pe.wait_ge(S_["q_done"], at(l, e))
                    for t in range(2):
                        mm = nc.tensor.matmul(bk[:, t * 2 * D:(t + 1) * 2 * D], h[:, e, (2 * i + t) * P:(2 * i + t + 1) * P],
                                              W[:, WKV:WKV + 2 * D], start=True, stop=True)
                    mm.then_inc(S_[st + "_full"], 1)
                elif st == "kvs":
                    pe.wait_ge(S_["k_done"], at(l, e))
                    for t in range(NT):
                        mm = nc.tensor.matmul(Bk[:, 0:D + 1], kf[:, e, t, :], kv[:, e, t, D:2 * D + 1], start=(t == 0), stop=(t == NT - 1))
                    mm.then_inc(S_["kvs_full"], 1)
                elif st == "att":
                    pe.wait_ge(S_["kvm_done"], at(l, e, 2, 1))
                    for t in range(NT):
                        bk = (A, Bk)[t // 2]
                        mm = nc.tensor.matmul(bk[:, (t % 2) * (D + LH):(t % 2 + 1) * (D + LH)], q[:, e, t * P:(t + 1) * P], kvm[:, e, :],
                                              start=True, stop=True)
                    mm.then_inc(S_["att_full"], 1)
                elif st == "atT":
                    pe.wait_ge(S_["at_done"], at(l, e))
                    for t in range(NT):
                        mm = nc.tensor.transpose(A[:, t * P:(t + 1) * P], z[:, e, t, :], ident)
                    mm.then_inc(S_["atT_full"], 1)
                elif st == "o":
                    pe.wait_ge(S_["atT_done"], at(l, e))
                    nc.tensor.matmul(Bk, W[:, WO:WO + D], s[:, e, :], start=True, stop=True).then_inc(S_["o_full"], 1)
                elif st[0] == "f":
                    f, bk = int(st[1]), (A, Bk)[int(st[1]) % 2]
                    if f == 0:
                        pe.wait_ge(ln["1"]["done"], at(l, e))
                    elif f >= 2:
                        pe.wait_ge(S_[f"f{f - 2}_done"], at(l, e))
                    nc.tensor.matmul(bk, W[:, W1 + f * P:W1 + (f + 1) * P], h[:, e, :], start=True, stop=True).then_inc(S_[st + "_full"], 1)
                elif st[0] == "y":
                    f = int(st[1])
                    pe.wait_ge(S_[f"f{max(f, 2)}_done"], at(l, e))
                    mm = nc.tensor.matmul(A, W[:, W2 + f * D:W2 + (f + 1) * D], hid[:, e, f, :], start=(f == 0), stop=(f == LFC - 1))
                    if f == LFC - 1:
                        mm.then_inc(S_["y_full"], 1)
                elif st[:2] == "sT":
                    k = which(st)
                    if k == "1":
                        pe.wait_ge(S_["o_sum"], at(l, e))
                    elif k == "2":
                        pe.wait_ge(S_["y_sum"], at(l, e))
                    elif k == "out":
                        pe.wait_ge(ln["2"]["done"], at(LAYERS, e))
                    elif k == "exp":
                        pe.wait_ge(ln["out"]["done"], at(0, e))
                    src = {"in": xT, "out": h, "exp": xT}.get(k, s)
                    bk = A if k == "1" else Bk
                    for t in range(NT):
                        mm = nc.tensor.transpose(bk[:, t * P:(t + 1) * P], src[:, e, t * P:(t + 1) * P], ident)
                    mm.then_inc(ln[k]["full"], 1)
                else:
                    k = st[2:]
                    pe.wait_ge(ln[k]["z"], at(l, e))
                    bk = {"1": Bk}.get(k, A)
                    for t in range(NT):
                        mm = nc.tensor.transpose(bk[:, t * P:(t + 1) * P], z[:, e, t, :], ident)
                    mm.then_inc(ln[k]["zfull"], 1)

            run(pe, STEPS["tensor"], part)

        @block.scalar
        def _(act):
            def part(st, e, l, par):
                A, Bk = ps[:, 2 * e, :], ps[:, 2 * e + 1, :]
                col = lambda k: w[:, par, k:k + 1]
                if st == "q":
                    act.wait_ge(S_["q_full"], at(l, e))
                    nc.scalar.activation(ex[:, e, :], A, ACT.Exp, bias=col(BQ)).then_inc(S_["q_exp"], 1)
                elif st == "kv":
                    act.wait_ge(S_["kv_done"], at(l, e))
                    nc.scalar.activation(ex[:, e, :].rearrange("p (t d) -> p t d", d=D), kv[:, e, :, 0:D], ACT.Exp).then_inc(S_["k_exp"], 1)
                elif st == "atT":
                    act.wait_ge(S_["atT_full"], at(l, e))
                    nc.scalar.activation(s[:, e, :], A, ACT.Identity).then_inc(S_["atT_done"], 1)
                elif st[0] == "f":
                    f = int(st[1])
                    act.wait_ge(S_[st + "_full"], at(l, e))
                    nc.scalar.activation(hid[:, e, f, :], (A, Bk)[f % 2], ACT.Gelu, bias=col(LC1 + f)).then_inc(S_[st + "_done"], 1)
                elif st[:2] == "sT":
                    k = which(st)
                    bk = {"1": A}.get(k, Bk)
                    act.wait_ge(ln[k]["rstd"], at(l, e))
                    for t in range(NT):
                        ins = nc.scalar.activation(z[:, e, t, :], bk[:, t * P:(t + 1) * P], ACT.Identity,
                                                   bias=nm[:, e, t:t + 1], scale=rs[:, e, t:t + 1])
                    ins.then_inc(ln[k]["z"], 1)

            run(act, STEPS["scalar"], part)

        @block.gpsimd
        def _(pool):
            def part(st, e, l, par):
                if st in ("q", "kv"):
                    k = st[0]
                    pool.wait_ge(S_[k + "_exp"], at(l, e))
                    pool.sem_inc(g["pool_passed"], 1)
                    nc.gpsimd.tensor_scalar(ex[:, e, :], ex[:, e, :], 1.0, 0.0, ALU.min, ALU.max).then_inc(S_[k + "_clip"], 1)
                elif st[:2] == "sT":
                    k = which(st)
                    pool.wait_ge(ln[k]["var"], at(l, e))
                    nc.gpsimd.tensor_tensor(rs[:, e, :], ve[:, e, 0, :], nhalf[:], ALU.pow).then_inc(ln[k]["rs"], 1)
                    pool.wait_ge(ln[k]["rs"], at(l, e))
                    nc.gpsimd.tensor_tensor(nm[:, e, :], ve[:, e, 1, :], rs[:, e, :], ALU.mult).then_inc(ln[k]["rstd"], 1)

            run(pool, STEPS["gpsimd"], part)

        @block.vector
        def _(dve):
            nc.vector.memset(kv[:, :, :, 2 * D:2 * D + 1], 1.0).then_inc(S_["one_set"], 1)

            def part(st, e, l, par):
                A, Bk = ps[:, 2 * e, :], ps[:, 2 * e + 1, :]
                col = lambda k: w[:, par, k:k + 1]
                if st == "phiq":
                    if e == 0:
                        dve.wait_ge(w_in[par], (l - par) * 16 + 32)
                        nc.vector.tensor_scalar(bq1[:, par:par + 1], col(BQ), 1.0, None, ALU.add).then_inc(S_["bq1_done"], 1)
                        dve.wait_ge(S_["bq1_done"], l + 1)
                    dve.wait_ge(S_["q_clip"], at(l, e))
                    nc.vector.scalar_tensor_tensor(q[:, e, :], A, bq1[:, par:par + 1], ex[:, e, :], ALU.add, ALU.max).then_inc(S_["q_done"], 1)
                elif st == "phik":
                    dve.wait_ge(S_["k_clip"], at(l, e))
                    nc.vector.scalar_tensor_tensor(kf[:, e], kv[:, e, :, 0:D], 1.0, ex[:, e, :].rearrange("p (t d) -> p t d", d=D),
                                                   ALU.add, ALU.max).then_inc(S_["k_done"], 1)
                elif st in ("kva", "kvb"):
                    i, bk = (0, Bk) if st == "kva" else (1, A)
                    dve.wait_ge(S_[st + "_full"], at(l, e))
                    ins = nc.vector.tensor_tensor(kv[:, e, 2 * i:2 * i + 2, 0:2 * D], bk.rearrange("p (t d) -> p t d", d=2 * D),
                                                  bkv[:, par, :].unsqueeze(1).to_broadcast([P, 2, 2 * D]), ALU.add)
                    if i == 1:
                        ins.then_inc(S_["kv_done"], 1)
                elif st == "kvs":
                    dve.wait_ge(S_["kvs_full"], at(l, e))
                    nc.vector.tensor_tensor(kvm[:, e, 0:D], Bk[:, 0:D], consts[:, BLOCKS:BLOCKS + D], ALU.mult).then_inc(S_["kvm_done"], 1)
                    nc.vector.tensor_scalar(kvm[:, e, D:D + LH], consts[:, HSEL:HSEL + LH], Bk[:, D:D + 1], None, ALU.mult).then_inc(S_["kvm_done"], 1)
                elif st == "att":
                    dve.wait_ge(S_["att_full"], at(l, e))
                    both = [bk[:, 0:2 * (D + LH)].rearrange("p (t n) -> p t n", n=D + LH) for bk in (A, Bk)]
                    for i in range(2):
                        ins = nc.vector.tensor_scalar(dn[:, e, 2 * i:2 * i + 2, :], both[i][:, :, D:D + LH], 1e-6, None, ALU.add)
                    ins.then_inc(S_["den_done"], 1)
                    dve.wait_ge(S_["den_done"], at(l, e))
                    nc.vector.reciprocal(dn[:, e], dn[:, e]).then_inc(S_["rec_done"], 1)
                    dve.wait_ge(S_["rec_done"], at(l, e))
                    for i in range(2):
                        ins = nc.vector.tensor_tensor(z[:, e, 2 * i:2 * i + 2, :].rearrange("p t (a c) -> p t a c", c=LD),
                                                      both[i][:, :, 0:D].rearrange("p t (a c) -> p t a c", c=LD),
                                                      dn[:, e, 2 * i:2 * i + 2, :].unsqueeze(3).to_broadcast([P, 2, LH, LD]), ALU.mult)
                    ins.then_inc(S_["at_done"], 1)
                elif st in ("o", "y3"):
                    bk, bias = (Bk, LBO) if st == "o" else (A, LC2)
                    dve.wait_ge(S_[st[0] + "_full"], at(l, e))
                    ins = nc.vector.scalar_tensor_tensor(s[:, e, :], bk, col(bias), h[:, e, :], ALU.add, ALU.add)
                    ins.then_inc(S_[st[0] + "_sum"], 1)
                elif st[:2] == "sT":
                    k = which(st)
                    bk = {"1": A}.get(k, Bk)
                    dve.wait_ge(ln[k]["full"], at(l, e))
                    for t in range(NT):
                        ins = nc.vector.bn_stats(st6[:, e, t, :], bk[:, t * P:(t + 1) * P])
                    ins.then_inc(ln[k]["stats"], 1)
                    dve.wait_ge(ln[k]["stats"], at(l, e))
                    dve.sem_inc(g["dve_passed"], 1)
                    for t in range(NT):
                        ins = nc.vector.bn_aggr(mv[:, e, t, :], st6[:, e, t, :])
                    ins.then_inc(ln[k]["aggr"], 1)
                    dve.wait_ge(ln[k]["aggr"], at(l, e))
                    nc.vector.tensor_scalar(ve[:, e, 1, :], mv[:, e, :, 0], -1.0, None, ALU.mult)
                    nc.vector.tensor_scalar(ve[:, e, 0, :], mv[:, e, :, 1], 1e-5, None, ALU.add).then_inc(ln[k]["var"], 1)
                elif st[:2] == "zT":
                    k = st[2:]
                    bk = {"1": Bk}.get(k, A)
                    dve.wait_ge(ln[k]["zfull"], at(l, e))
                    if k == "out":
                        nc.vector.tensor_scalar(xg[:, e, :], xT[:, e, :], mods[:, 1, GB, e:e + 1], None, ALU.add).then_inc(xg_done, 1)
                        dve.wait_ge(xg_done, e + 1)
                        ins = nc.vector.scalar_tensor_tensor(xT[:, e, :], bk, mods[:, 1, GG, e:e + 1], xg[:, e, :], ALU.mult, ALU.add)
                    else:
                        a, c = {"exp": (mods[:, 1, CB, e:e + 1], mods[:, 1, SB, e:e + 1]), "in": (mods[:, 1, CA, e:e + 1], mods[:, 1, SA, e:e + 1]), "1": (col(LG1), col(LBE1)),
                                "2": (col(LG2), col(LBE2))}[k]
                        ins = nc.vector.tensor_scalar(h[:, e, :], bk, a, c, ALU.mult, ALU.add)
                    ins.then_inc(ln[k]["done"], 1)
                    if k == "2" and e == B - 1:
                        dve.wait_ge(ln[k]["done"], at(l + 1, e))
                        nc.vector.tensor_copy(dn[:, e, 0, 0:1], dn[:, e, 0, 1:2]).then_inc(w_free, 1)

            run(dve, STEPS["vector"], part)


def experts1(nc, g):
    ps, consts, mods, xT, ident = (g[k] for k in ("ps", "consts", "mods", "xT", "ident"))
    rw, gu, dn1, w1_in, h = (g[k] for k in ("rw", "gu", "dn1", "w1_in", "h"))
    KF, NB = len(FCH), B * NT
    with ExitStack() as ctx:
        def sb(name, shape, dt=F32):
            return ctx.enter_context(nc.sbuf_tensor(name, shape, dt))

        def sem(name):
            return ctx.enter_context(nc.semaphore(name))

        hi, lo = sb("gu_high", [P, U, 2, FF1], F32R), sb("gu_low", [P, U, 2, FF1], F32R)
        hh, hl = sb("h_high", [P, B, S], F32R), sb("h_low", [P, B, S], F32R)
        sg = sb("e_silu", [P, 2, S])
        hid = sb("e_hid", [P, 2, KF, S])
        acc = sb("e_acc", [P, NT, D])
        outb = sb("e_out", [P, NT, D])
        fin = sb("e_fin", [P, S])
        pb = sb("e_probs", [P, NB, E])
        mx = sb("e_max", [P, NB])
        total = sb("e_sum", [P, NB])
        inv = sb("e_inv", [P, NB])
        mx8 = sb("e_mx8", [P, NB, 8])
        ix8 = sb("e_ix8", [P, NB, 8], U32)
        ixf = sb("e_ixf", [P, NB, 8])
        tv = sb("e_tv", [P, NB, 2])
        eq = sb("e_eq", [P, 2, NB, E])
        wt = sb("e_wt", [P, NB, E])
        wcur = sb("e_wcur", [P, NT, E])

        rt_full, m_done, pe_done = sem("router_full"), sem("router_max"), sem("router_exp")
        hh_done, split_done = sem("h_high_done"), sem("h_split")
        whi_done, wsplit_done = sem("w_high_done"), sem("w_split")
        g_full, u_full, s_done, h_done = sem("g_full"), sem("u_full"), sem("silu_done1"), sem("hid_done1")
        y_full, acc_done, w_done = sem("y_full1"), sem("acc_done1"), sem("wcur_done")
        aT_full, fin_done, fT_full = sem("aT_full"), sem("fin_done"), sem("fT_full")
        out_done, stored, dch = sem("out_done"), sem("stored"), sem("e_chain")
        NH = U * KF

        def phases(eng, phase, finish):
            phase(0, True)
            with eng.Fori(1, B) as b:
                phase(b, False)
            for step in finish:
                step(B - 1)

        block = ctx.enter_context(nc.Block())

        @block.sync
        def _(sp):
            with sp.Fori(0, B) as b:
                sp.wait_ge(out_done, b + 1)
                sp.sem_inc(g["sp_passed"], 1)
                sp.dma_start(g["out_tok"][b], outb[:]).then_inc(stored, 16)
            sp.wait_ge(stored, 16 * B)

        @block.tensor
        def _(pe):
            pe.wait_ge(w1_in, 80)

            def router():
                for e in range(B):
                    for t in range(NT):
                        at = (e * NT + t) * E
                        mm = nc.tensor.matmul(ps[:, 4, at:at + E], h[:, e, t * P:(t + 1) * P], rw[:], start=True, stop=True)
                mm.then_inc(rt_full, 1)

            def acc_turn(b):
                pe.wait_ge(acc_done, b * U + U)
                for t in range(NT):
                    mm = nc.tensor.transpose(ps[:, 4, t * P:(t + 1) * P], acc[:, t, :], ident)
                mm.then_inc(aT_full, 1)

            def fin_turn(b):
                pe.wait_ge(fin_done, b + 1)
                for t in range(NT):
                    mm = nc.tensor.transpose(ps[:, 5, t * P:(t + 1) * P], fin[:, t * P:(t + 1) * P], ident)
                mm.then_inc(fT_full, 1)

            def phase(b, first):
                hb = [x[:, bass.ds(b, 1), :].rearrange("p o s -> p (o s)") for x in (hh, hl)]

                def hidden(n):
                    if first:
                        pe.wait_ge(wsplit_done, n + 1)
                    for k, (a, m) in enumerate(FCH):
                        i = n * KF + k
                        if i >= 2:
                            pe.wait_ge(h_done, b * NH + (i - 1))
                        for which, full in ((0, g_full), (1, u_full)):
                            to = ps[0:m, 2 * which + i % 2, :]
                            nc.tensor.matmul(to, hi[:, n, which, a:a + m], hb[0], start=True, stop=False)
                            nc.tensor.matmul(to, lo[:, n, which, a:a + m], hb[0], start=False, stop=False)
                            nc.tensor.matmul(to, hi[:, n, which, a:a + m], hb[1], start=False, stop=True).then_inc(full, 1)

                def expert_out(n):
                    pe.wait_ge(h_done, b * NH + (n * KF + KF))
                    if n >= 2:
                        pe.wait_ge(acc_done, b * U + (n - 1))
                    for t in range(NT):
                        for k, (a, m) in enumerate(FCH):
                            mm = nc.tensor.matmul(ps[:, 6 + n % 2, t * P:(t + 1) * P], hid[0:m, n % 2, k, t * P:(t + 1) * P],
                                                  dn1[0:m, k, n, :], start=(k == 0), stop=(k == KF - 1))
                    mm.then_inc(y_full, 1)

                if first:
                    pe.wait_ge(split_done, 1)
                hidden(0)
                if first:
                    router()
                else:
                    acc_turn(b - 1)
                hidden(1)
                if not first:
                    fin_turn(b - 1)
                if not first:
                    pe.wait_ge(acc_done, b * U)
                expert_out(0)
                for n in range(2, U):
                    hidden(n)
                    expert_out(n - 1)
                expert_out(U - 1)

            phases(pe, phase, (acc_turn, fin_turn))

        @block.scalar
        def _(act):
            def weights(n):
                nc.scalar.activation(hi[:, n], gu[:, n], ACT.Identity).then_inc(whi_done, 1)

            act.wait_ge(w1_in, 80)
            for e in range(B):
                nc.scalar.activation(hh[:, e, :], h[:, e, :], ACT.Identity).then_inc(hh_done, 1)
                if e == 0:
                    weights(0)
            weights(1)

            def phase(b, first):
                for n in range(U):
                    if first and n + 2 < U:
                        weights(n + 2)
                    for k, (a, m) in enumerate(FCH):
                        i = n * KF + k
                        act.wait_ge(g_full, b * NH + (i + 1))
                        if i >= 2:
                            act.wait_ge(h_done, b * NH + (i - 1))
                        nc.scalar.activation(sg[0:m, i % 2, :], ps[0:m, i % 2, :], ACT.Silu).then_inc(s_done, 1)
                    if first and n == 0:
                        act.wait_ge(m_done, 1)
                        nc.scalar.activation(pb[:], pb[:], ACT.Exp).then_inc(pe_done, 1)

            phases(act, phase, ())

        @block.vector
        def _(dve):
            steps = [0]

            def then(ins):
                steps[0] += 1
                ins.then_inc(dch, 1)
                dve.wait_ge(dch, steps[0])

            def weights(n):
                dve.wait_ge(whi_done, n + 1)
                nc.vector.tensor_tensor(lo[:, n], gu[:, n], hi[:, n].bitcast(F32), ALU.subtract).then_inc(wsplit_done, 1)

            def low(e):
                dve.wait_ge(hh_done, e + 1)
                nc.vector.tensor_tensor(hl[:, e, :], h[:, e, :], hh[:, e, :].bitcast(F32), ALU.subtract).then_inc(split_done, 1)

            low(0)
            weights(0)
            weights(1)
            for e in range(1, B):
                low(e)

            def router_max():
                dve.wait_ge(rt_full, 1)
                src = ps[:, 4, 0:NB * E].rearrange("p (t e) -> p t e", e=E)
                then(nc.vector.tensor_reduce(mx[:], src, AX, ALU.max))
                nc.vector.tensor_tensor(pb[:], src, mx[:].unsqueeze(2).to_broadcast([P, NB, E]), ALU.subtract).then_inc(m_done, 1)

            def gates(part):
                half = range(NB // 2) if part in (1, 3) else range(NB // 2, NB)
                if part == 0:
                    dve.wait_ge(pe_done, 1)
                    then(nc.vector.tensor_reduce(total[:], pb[:], AX, ALU.add))
                    then(nc.vector.reciprocal(inv[:], total[:]))
                    then(nc.vector.tensor_tensor(pb[:], pb[:], inv[:].unsqueeze(2).to_broadcast([P, NB, E]), ALU.mult))
                elif part in (1, 2):
                    for t in half:
                        ins = nc.vector.max(mx8[:, t, :], pb[:, t, :])
                    then(ins)
                elif part in (3, 4):
                    for t in half:
                        ins = nc.vector.max_index(ix8[:, t, :], mx8[:, t, :], pb[:, t, :])
                    then(ins)
                elif part == 5:
                    then(nc.vector.tensor_tensor(mx[:], mx8[:, :, 0], mx8[:, :, 1], ALU.add))
                    then(nc.vector.tensor_scalar(total[:], mx[:], 1e-20, None, ALU.add))
                    nc.vector.tensor_copy(ixf[:], ix8[:])
                    then(nc.vector.reciprocal(inv[:], total[:]))
                    then(nc.vector.tensor_tensor(tv[:], mx8[:, :, 0:2], inv[:].unsqueeze(2).to_broadcast([P, NB, 2]), ALU.mult))
                    iota = consts[:, IOTA:IOTA + E].unsqueeze(1).to_broadcast([P, NB, E])
                    for i in range(2):
                        ins = nc.vector.tensor_tensor(eq[:, i], iota, ixf[:, :, i:i + 1].to_broadcast([P, NB, E]), ALU.is_equal)
                    then(ins)
                    for i in range(2):
                        ins = nc.vector.tensor_tensor(eq[:, i], eq[:, i], tv[:, :, i:i + 1].to_broadcast([P, NB, E]), ALU.mult)
                    then(ins)
                    then(nc.vector.tensor_tensor(wt[:], eq[:, 0], eq[:, 1], ALU.add))

            def finish(b):
                dve.wait_ge(aT_full, b + 1)
                at = (lambda x: x[:, b:b + 1]) if isinstance(b, int) else (lambda x: x[:, bass.ds(b, 1)])
                nc.vector.scalar_tensor_tensor(fin[:], ps[:, 4, :], at(mods[:, 1, GX, :]), at(xT[:]).rearrange("p o s -> p (o s)"),
                                               ALU.mult, ALU.add).then_inc(fin_done, 1)

            def output(b, again=True):
                dve.wait_ge(fT_full, b + 1)
                if again:
                    dve.wait_ge(stored, b * 16)
                nc.vector.tensor_copy(outb[:].rearrange("p t d -> p (t d)"), ps[:, 5, :]).then_inc(out_done, 1)

            def phase(b, first):
                def gated(n):
                    for k, (a, m) in enumerate(FCH):
                        i = n * KF + k
                        if n >= 2 and k == 0:
                            dve.wait_ge(y_full, b * U + (n - 1))
                        dve.wait_ge(u_full, b * NH + (i + 1))
                        dve.wait_ge(s_done, b * NH + (i + 1))
                        nc.vector.tensor_tensor(hid[0:m, n % 2, k, :], ps[0:m, 2 + i % 2, :], sg[0:m, i % 2, :], ALU.mult).then_inc(h_done, 1)
                        if first and n in (1, 2):
                            gates((n - 1) * KF + k)

                def accumulate(n):
                    dve.wait_ge(y_full, b * U + (n + 1))
                    y = ps[:, 6 + n % 2, :]
                    if n == 0:
                        ins = nc.vector.tensor_copy(acc[:].rearrange("p t d -> p (t d)"), y)
                    else:
                        for t in range(NT):
                            ins = nc.vector.scalar_tensor_tensor(acc[:, t, :], y[:, t * P:(t + 1) * P], wcur[:, t, n - 1:n],
                                                                 acc[:, t, :], ALU.mult, ALU.add)
                    ins.then_inc(acc_done, 1)
                    dve.wait_ge(acc_done, b * U + (n + 1))

                gated(0)
                if first:
                    router_max()
                    weights(2)
                else:
                    finish(b - 1)
                gated(1)
                if not first:
                    output(b - 1)
                accumulate(0)
                for n in range(2, U):
                    if first and n + 1 < U:
                        weights(n + 1)
                    gated(n)
                    if n == 2:
                        nc.vector.tensor_copy(wcur[:], wt[:, bass.ds(b * NT, NT), :]).then_inc(w_done, 1)
                        dve.wait_ge(w_done, b + 1)
                    accumulate(n - 1)
                accumulate(U - 1)

            phases(dve, phase, (finish, output))


def _layout(i):
    def cols(a):
        return np.ascontiguousarray(np.asarray(a).reshape(-1, P).T)

    a = {k: np.asarray(v) for k, v in i.items()}
    eye = np.eye(P, dtype=np.float32)
    blocks = np.kron(np.eye(LH), np.ones((LD, LD))).astype(np.float32)
    hsel = np.kron(np.eye(LH), np.ones((LD, 1))).astype(np.float32)
    iota = np.tile(np.arange(E, dtype=np.float32), (P, 1))
    pick = np.tile((np.arange(2 * E - 1) == E - 1).astype(np.float32), (P, 1))
    consts = np.concatenate([eye, blocks, hsel, iota, np.ones((P, P), np.float32), pick], 1)
    vecs = np.concatenate([cols(a[k]) for k in (
        "L0_attn_b_out", "L0_attn_ln_gamma", "L0_attn_ln_beta", "L0_ffn_gate_bi", "L0_ffn_exp_bi",
        "L1_attn_gf", "L1_attn_bef", "L0_c", "L1_c")], 1)

    def chunks(w):
        w = w.reshape(w.shape[:-2] + (w.shape[-2] // P, P, w.shape[-1]))
        return np.ascontiguousarray(np.moveaxis(w, -2, 0))

    lw = np.concatenate(
        [a["L1_attn_Wq"], a["L1_attn_Wk"], a["L1_attn_Wv"], a["L1_attn_Wo"], a["L1_attn_W1"],
         np.moveaxis(a["L1_attn_W2"].reshape(LAYERS, LFC, P, D), 1, 2).reshape(LAYERS, P, LFC * D)]
        + [np.moveaxis(a[k].reshape(LAYERS, -1, P), 1, 2) for k in (
            "L1_attn_bq", "L1_attn_bo", "L1_attn_g1", "L1_attn_be1", "L1_attn_g2", "L1_attn_be2",
            "L1_attn_c1", "L1_attn_c2")], 2)
    gate = np.concatenate([a["L1_ffn_shared_gate"][None], a["L1_ffn_expert_gate"]])
    up = np.concatenate([a["L1_ffn_shared_up"][None], a["L1_ffn_expert_up"]])
    down = np.concatenate([a["L1_ffn_shared_down"][None], a["L1_ffn_expert_down"]])
    gu = np.stack([np.transpose(gate, (2, 0, 1)), np.transpose(up, (2, 0, 1))], 2)
    return {
        "x": a["L0_attn_x"], "vecs": vecs, "consts": consts,
        "wmod": np.stack([a["L0_wmod"], a["L1_wmod"]], 1),
        "wqkv": a["L0_attn_w_qkv"].reshape(D, 3, HEADS * DH),
        "wout": chunks(a["L0_attn_w_out"]),
        "gwi": a["L0_ffn_gate_wi"], "gwo": chunks(a["L0_ffn_gate_wo"]), "gbo": a["L0_ffn_gate_bo"],
        "ewi": np.transpose(a["L0_ffn_exp_wi"], (1, 0, 2)), "ewo": chunks(a["L0_ffn_exp_wo"]),
        "ebo": a["L0_ffn_exp_bo"],
        "lw": lw, "bkv": np.concatenate([a["L1_attn_bk"], a["L1_attn_bv"]], 1),
        "rw": a["L1_ffn_gate_w"].T, "gu": gu, "dn": np.transpose(down, (2, 0, 1)),
    }


def kernel(**inputs):
    from concourse import bacc
    from concourse.bass_utils import run_bass_kernel_spmd

    nc = bacc.Bacc("TRN2", target_bir_lowering=False, num_devices=1)
    arrays = {f"in_{k}": np.ascontiguousarray(v) for k, v in _layout(inputs).items()}
    ins = {k[3:]: nc.dram_tensor(k, v.shape, mybir.dt.from_np(v.dtype), kind="ExternalInput").ap()
           for k, v in arrays.items()}
    out = nc.dram_tensor("out_x", (B, S, D), F32, kind="ExternalOutput").ap()
    build(nc, ins, out)
    r = run_bass_kernel_spmd(nc, [arrays], core_ids=[0])
    return r.results[0]["out_x"]
```
